# Optimizing a Trainium2 kernel written in Bass

```python
import numpy as np
import jax
import jax.numpy as jnp

def _softmax(x, axis=-1):
    return jax.nn.softmax(x, axis=axis)

def _gelu(x):
    return jax.nn.gelu(x, approximate=True)

def _silu(x):
    return jax.nn.silu(x)

def _sigmoid(x):
    return jax.nn.sigmoid(x)

def _layernorm(x, axis=-1, eps=1e-05):
    m = jnp.mean(x, axis=axis, keepdims=True)
    v = jnp.var(x, axis=axis, keepdims=True)
    return (x - m) / jnp.sqrt(v + eps)

def _scatter_add(tgt, idx, src, axis=0):
    return tgt.at[idx].add(src)

def _segment_sum(src, seg, n):
    return jax.ops.segment_sum(src, seg, n)
kernel_name = 'mk_seq_preln_d1_jaxref_r8_fa7e70'

def setup_inputs(seed: int=0):
    np.random.seed(seed)
    _w = jnp.asarray

    def _L0_attn_setup():
        import jax, jax.numpy as jnp
        import numpy as np
        D = 128
        H = 16
        DH = D // H
        B, N = (4, 128)
        key = jax.random.key(seed)
        k0, k1, k2 = jax.random.split(key, 3)
        x = jax.random.normal(k0, (B, N, D), jnp.float32)
        Wkqv = jax.random.normal(k1, (H, D, 2 * D + DH), jnp.float32) * 0.02
        bkqv = jnp.zeros((H, 2 * D + DH), jnp.float32)
        Wp = jax.random.normal(k2, (D, D), jnp.float32) * 0.02
        bp = jnp.zeros((D,), jnp.float32)
        return {'x': x, 'Wkqv': Wkqv, 'bkqv': bkqv, 'Wp': Wp, 'bp': bp}
    _L0_attn_in = _L0_attn_setup()

    def _L0_ffn_setup():
        import jax, jax.numpy as jnp
        import numpy as np
        B, S, H = (2, 256, 128)
        E_ROUTED = 8
        TOP_K = 2
        I = 256
        key = jax.random.key(seed)
        ks = jax.random.split(key, 9)
        s = 0.02
        return {'x': jax.random.normal(ks[0], (B, S, H), dtype=jnp.float32), 'shared_gate': jax.random.normal(ks[1], (I, H), dtype=jnp.float32) * s, 'shared_up': jax.random.normal(ks[2], (I, H), dtype=jnp.float32) * s, 'shared_down': jax.random.normal(ks[3], (H, I), dtype=jnp.float32) * s, 'gate_w': jax.random.normal(ks[4], (E_ROUTED, H, I), dtype=jnp.float32) * s, 'up_w': jax.random.normal(ks[5], (E_ROUTED, H, I), dtype=jnp.float32) * s, 'down_w': jax.random.normal(ks[6], (E_ROUTED, I, H), dtype=jnp.float32) * s, 'router_w': jax.random.normal(ks[7], (E_ROUTED, H), dtype=jnp.float32) * s, 'routing_bias': jnp.zeros((E_ROUTED,), dtype=jnp.float32)}
    _L0_ffn_in = _L0_ffn_setup()
    _d = {'L0_attn_x': _L0_attn_in['x'], 'L0_attn_Wkqv': _L0_attn_in['Wkqv'], 'L0_attn_bkqv': _L0_attn_in['bkqv'], 'L0_attn_Wp': _L0_attn_in['Wp'], 'L0_attn_bp': _L0_attn_in['bp'], 'L0_ffn_shared_gate': _L0_ffn_in['shared_gate'], 'L0_ffn_shared_up': _L0_ffn_in['shared_up'], 'L0_ffn_shared_down': _L0_ffn_in['shared_down'], 'L0_ffn_gate_w': _L0_ffn_in['gate_w'], 'L0_ffn_up_w': _L0_ffn_in['up_w'], 'L0_ffn_down_w': _L0_ffn_in['down_w'], 'L0_ffn_router_w': _L0_ffn_in['router_w'], 'L0_ffn_routing_bias': _L0_ffn_in['routing_bias']}
    _x0 = _d['L0_attn_x']
    _d['L0_attn_x'] = jax.random.normal(jax.random.fold_in(jax.random.key(seed), 1), (8, 512, 128), dtype=_x0.dtype)
    del _x0
    return _d

def reference(L0_attn_x, L0_attn_Wkqv, L0_attn_bkqv, L0_attn_Wp, L0_attn_bp, L0_ffn_shared_gate, L0_ffn_shared_up, L0_ffn_shared_down, L0_ffn_gate_w, L0_ffn_up_w, L0_ffn_down_w, L0_ffn_router_w, L0_ffn_routing_bias):

    def _L0_attn_ref(x, Wkqv, bkqv, Wp, bp):
        import jax, jax.numpy as jnp
        import numpy as np
        D = 128
        H = 16
        DH = D // H
        B, N = (4, 128)
        Bm, Nm, Dm = x.shape
        y = jnp.einsum('bnd,hde->bhne', x, Wkqv) + bkqv[None, :, None, :]
        k = y[..., :Dm]
        q = y[..., Dm:2 * Dm]
        v = y[..., 2 * Dm:]
        A = jnp.einsum('bhnd,bhmd->bhnm', q, k) / jnp.sqrt(jnp.float32(Dm))
        mask = jnp.tril(jnp.ones((Nm, Nm), dtype=bool))
        A = jnp.where(mask[None, None], A, -jnp.inf)
        A = jax.nn.softmax(A, axis=-1)
        sa = jnp.einsum('bhnm,bhmd->bnhd', A, v).reshape(Bm, Nm, Dm)
        return sa @ Wp + bp

    def _L0_ffn_ref(x, shared_gate, shared_up, shared_down, gate_w, up_w, down_w, router_w, routing_bias):
        import jax, jax.numpy as jnp
        import numpy as np
        B, S, H = (2, 256, 128)
        E_ROUTED = 8
        TOP_K = 2
        I = 256
        b, s, h = x.shape
        shared = jnp.einsum('bsi,hi->bsh', jax.nn.silu(jnp.einsum('bsh,ih->bsi', x, shared_gate)) * jnp.einsum('bsh,ih->bsi', x, shared_up), shared_down)
        logits = jnp.einsum('bsh,eh->bse', x, router_w) + routing_bias
        probs = jax.nn.sigmoid(logits)
        scores, indices = jax.lax.top_k(probs, TOP_K)
        scores = scores / jnp.sum(scores, axis=-1, keepdims=True)
        t = b * s
        xf = x.reshape(t, h)
        idx = indices.reshape(t, TOP_K)
        sc = scores.reshape(t, TOP_K)
        w = jnp.zeros((t, E_ROUTED), dtype=x.dtype)
        w = w.at[jnp.arange(t)[:, None], idx].add(sc)
        g = jax.nn.silu(jnp.einsum('th,ehi->tei', xf, gate_w))
        u = jnp.einsum('th,ehi->tei', xf, up_w)
        combined = jnp.einsum('tei,eih,te->th', g * u, down_w, w)
        return shared + combined.reshape(b, s, h)
    x = L0_attn_x
    x = x + _L0_attn_ref(_layernorm(x, axis=-1), L0_attn_Wkqv, L0_attn_bkqv, L0_attn_Wp, L0_attn_bp)
    x = x + _L0_ffn_ref(_layernorm(x, axis=-1), L0_ffn_shared_gate, L0_ffn_shared_up, L0_ffn_shared_down, L0_ffn_gate_w, L0_ffn_up_w, L0_ffn_down_w, L0_ffn_router_w, L0_ffn_routing_bias)
    return x

_drawn_inputs = setup_inputs


def setup_inputs(seed=0):
    import zlib

    import numpy as np

    out = dict(_drawn_inputs(seed))
    spreads = {'L0_attn_bkqv': (0.0, 0.351), 'L0_attn_bp': (0.0, 0.1), 'L0_ffn_routing_bias': (0.0, 0.8)}
    factors = {'L0_attn_Wkqv': 8.0,
     'L0_ffn_shared_gate': 6.671,
     'L0_ffn_shared_up': 6.474,
     'L0_ffn_shared_down': 6.428,
     'L0_ffn_gate_w': 8.0,
     'L0_ffn_up_w': 8.0,
     'L0_ffn_down_w': 8.0,
     'L0_ffn_router_w': 8.0}
    for name, (base, spread) in spreads.items():
        noise = np.random.default_rng([zlib.crc32(name.encode()), seed]).standard_normal(out[name].shape)
        drawn = base * np.exp(spread * noise) if base else spread * noise
        out[name] = jnp.asarray(drawn.astype(out[name].dtype))
    for name, factor in factors.items():
        out[name] = (out[name] * factor).astype(out[name].dtype)
    return out
```

```python
import concourse.bass as bass
from concourse import mybir
import numpy as np
from contextlib import ExitStack

F32 = mybir.dt.float32
F32R = mybir.dt.float32r
BF16 = mybir.dt.bfloat16
I32 = mybir.dt.int32
ALU = mybir.AluOpType
ACT = mybir.ActivationFunctionType
AX = mybir.AxisListType

P = 128
B, N, D = 8, 512, 128
H, DH = 16, 8
E, I = 8, 256
TB = N // P
TOK = B * N
TILES = B * TB
KQV = 2 * D + DH
V1 = DH + 1
EW = 2 * I + 2 * D
SCALE = float(D) ** -0.5
EPS = 1e-5
MASKED = -1e30
RSQRT_MAGIC = float(0x5F3759DF)


def f(ap):
    return ap.bitcast(F32)


def seg(i, n, width=None):
    width = n if width is None else width
    return slice(i * n, i * n + width) if isinstance(i, int) else bass.ds(i * n, width)


def one_of(i):
    return slice(i, i + 1) if isinstance(i, int) else bass.ds(i, 1)


def tiles(nc, ctx):
    return lambda name, shape, dtype: ctx.enter_context(nc.sbuf_tensor(name, shape, dtype))


def positive(value):
    return not isinstance(value, int) or value > 0


def carry(eng, m):
    m.carriers += 1
    eng.memset(m.carrier[:, m.carriers:m.carriers + 1], 0.0)


def loop(eng, turns, body):
    body(0)
    with eng.Fori(1, turns) as t:
        body(t)


class Chain:

    def __init__(self, eng, sem, turn, per):
        self.eng, self.sem, self.base, self.n, self.per = eng, sem, turn * per, 0, per

    def link(self, ins):
        ins.then_inc(self.sem, 1)
        self.n += 1
        self.eng.wait_ge(self.sem, self.base + self.n)

    def end(self):
        assert self.n == self.per, (self.n, self.per)


def rsqrt_steps(nc, link, v, y, t):
    link(nc.vector.tensor_scalar(v, v, EPS, None, ALU.add))
    link(nc.vector.tensor_scalar(t.bitcast(I32), v.bitcast(I32), 1, None, ALU.logical_shift_right))
    link(nc.vector.tensor_scalar(y.bitcast(I32), t.bitcast(I32), -1.0, RSQRT_MAGIC, ALU.mult, ALU.add))
    for _ in range(4):
        link(nc.vector.tensor_tensor(t, y, y, ALU.mult))
        link(nc.vector.tensor_tensor(t, t, v, ALU.mult))
        link(nc.vector.tensor_scalar(t, t, -0.5, 1.5, ALU.mult, ALU.add))
        link(nc.vector.tensor_tensor(y, y, t, ALU.mult))


RSQRT_LINKS = 3 + 4 * 4


class Mem:

    def __init__(self, nc, io):
        (self.x, self.Wkqv, self.bkqv, self.Wp, self.bp, self.shared_gate, self.shared_up, self.shared_down, self.gate_w,
         self.up_w, self.down_w, self.router_w, self.routing_bias, self.out, self.w_dram) = io
        sb = nc.alloc_sbuf_tensor
        self.carrier = sb("carrier", [P, 64], F32)
        self.carriers = 0
        self.ident = sb("ident", [P, P], F32)
        self.ident_b = sb("ident_b", [P, P], BF16)
        self.mask_b = sb("mask_b", [P, P], BF16)
        self.bv_bc = sb("bv_bc", [P, H, DH], F32)
        self.bp_bc = sb("bp_bc", [P, D], F32)
        self.rb_bc = sb("rb_bc", [P, E], F32)
        self.order = sb("order", [P, 2 * TB, E], F32)
        self.x_sb = sb("x_sb", [P, TILES, D], F32)
        self.xh = sb("xh", [P, TOK], F32R)
        self.xl = sb("xl", [P, TOK], F32R)
        self.v_sb = sb("v_sb", [P, TILES, H * V1], F32)
        self.stats = sb("stats", [P, TILES, 2], F32)
        self.rstd = sb("rstd", [P, TILES], F32)
        self.mh = sb("mh", [P, H, D], F32R)
        self.ml = sb("ml", [P, H, D], F32R)
        self.bq = sb("bq", [P, H], F32)
        self.wv = sb("wv", [P, H * DH], F32)
        self.wp = sb("wp", [P, D], F32)
        self.rwT = sb("rwT", [P, E], F32)
        self.wraw = sb("wraw", [P, 2, EW], F32)
        self.wh = [sb(f"wh{s}", [P, EW], F32R) for s in range(2)]
        self.wl = [sb(f"wl{s}", [P, EW], F32R) for s in range(2)]
        self.psum = [nc.alloc_psum_tensor(f"bank{i}", [P, 512], F32) for i in range(8)]
        self.o_sb = sb("o_sb", [P, TILES, H * V1], F32)


def prepare(nc, m, ctx):
    sb, sem = tiles(nc, ctx), nc.alloc_semaphore
    HG = 2
    wst = sb("wst", [P, 2, HG, KQV], F32)
    wT = sb("wT", [P, 2, 2 * D], F32)
    bias_rows = sb("bias_rows", [H, KQV], F32)
    bqT = sb("bqT", [P, H], F32)
    rw_rows = sb("rw_rows", [E, D], F32)
    sh_rows = sb("sh_rows", [P, 3, I], F32)
    bn = sb("bn", [P, TILES, 6], F32)
    tmp = sb("tmp_rstd", [P, TILES], F32)
    var = sb("var", [P, TILES], F32)

    x_loaded = sem("x_loaded")
    small_loaded = sem("small_loaded")
    shared_loaded = sem("shared_loaded")
    head_loaded = [sem(f"head_loaded{s}") for s in range(2)]
    ident_made = sem("ident_made")
    consts = sem("consts")
    wv_copied = sem("wv_copied")
    bias_T = sem("bias_T")
    bias_copied = sem("bias_copied")
    w_T = sem("w_T")
    w_copied = sem("w_copied")
    m_done = sem("m_done")
    mh_ready = sem("mh_ready")
    ml_ready = sem("ml_ready")
    shared_T = sem("shared_T")
    shared_copied = sem("shared_copied")
    dve_chain = sem("dve_chain0")

    with nc.Block() as block:

        @block.sync
        def _(sp):
            sp.dma_start(bias_rows[:, :], m.bkqv).then_inc(small_loaded, 16)
            sp.dma_start(rw_rows[:, :], m.router_w).then_inc(small_loaded, 16)
            sp.dma_start(m.bv_bc[:, :, :], m.bkqv[:, 2 * D:KQV].partition_broadcast(P)).then_inc(small_loaded, 16)
            sp.dma_start(m.bp_bc[:, :], m.bp.partition_broadcast(P)).then_inc(small_loaded, 16)
            sp.dma_start(m.rb_bc[:, :], m.routing_bias.partition_broadcast(P)).then_inc(small_loaded, 16)
            sp.dma_start(m.wp[:, :], m.Wp).then_inc(small_loaded, 16)
            for n in range(H // HG):
                if n >= 2:
                    sp.wait_ge(m_done, (n - 1) * HG)
                    sp.wait_ge(wv_copied, n - 1)
                sp.dma_start(wst[:, n % 2, :, :], m.Wkqv[n * HG:(n + 1) * HG, :, :].rearrange("h d e -> d h e")).then_inc(head_loaded[n % 2], 16)
            sp.wait_ge(small_loaded, 16 * 6)

        @block.scalar
        def _(act):
            with act.Fori(0, B) as b:
                act.dma_start(m.x_sb[:, bass.ds(b * TB, TB), :], m.x[bass.ds(b, 1), :, :].rearrange("b (t p) d -> p (b t) d", p=P)).then_inc(x_loaded, 16)
            for k in range(2):
                act.dma_start(sh_rows[:, k, :].rearrange("p (t d) -> p t d", t=2), (m.shared_gate, m.shared_up)[k].rearrange("(t p) d -> p t d", p=P)).then_inc(shared_loaded, 16)
            act.dma_start(sh_rows[:, 2, :], m.shared_down).then_inc(shared_loaded, 16)
            act.wait_ge(bias_T, 1)
            nc.scalar.activation(bqT[:, :], m.psum[6][:, 0:H], ACT.Copy)
            nc.scalar.activation(m.rwT[:, :], m.psum[6][:, H:H + E], ACT.Copy).then_inc(bias_copied, 1)
            def turn(t):
                for k in range(4):
                    act.wait_ge(w_T, t * 4 + k + 1)
                    if positive(t * 4 + k - 1):
                        act.wait_ge(m_done, t * 4 + k - 1)
                    nc.scalar.activation(wT[:, k % 2, :], m.psum[k % 2][:, 0:2 * D], ACT.Copy).then_inc(w_copied, 1)
                    act.wait_ge(m_done, t * 4 + k + 1)
                    nc.scalar.activation(m.mh[:, bass.ds(t * 4 + k, 1), :], m.psum[2 + k % 2][:, 0:D], ACT.Copy, scale=SCALE).then_inc(mh_ready, 1)
            loop(act, H // (2 * HG), turn)
            for k in range(2):
                act.wait_ge(shared_T, k + 1)
                nc.scalar.activation(m.wraw[:, 0, k * 512:min(EW, k * 512 + 512)], m.psum[4 + k][:, 0:min(512, EW - k * 512)], ACT.Copy).then_inc(shared_copied, 1)
            act.wait_ge(x_loaded, 16 * B)

        @block.gpsimd
        def _(pool):
            nc.gpsimd.memset(m.carrier[:, 0:1], 0.0)
            nc.gpsimd.memset(m.ident[:, :], 0.0).then_inc(consts, 1)
            nc.gpsimd.memset(m.ident_b[:, :], 0.0).then_inc(consts, 1)
            nc.gpsimd.memset(m.mask_b[:, :], 0.0).then_inc(consts, 1)
            pool.wait_ge(consts, 3)
            for t in (m.ident, m.ident_b):
                nc.gpsimd.affine_select(out=t[:, :], in_=t[:, :], compare_op=ALU.not_equal, fill=1.0, base=0, pattern=[[-1, P]], channel_multiplier=1).then_inc(ident_made, 1)
            nc.gpsimd.affine_select(out=m.mask_b[:, :], in_=m.mask_b[:, :], compare_op=ALU.is_ge, fill=MASKED, base=0, pattern=[[-1, P]], channel_multiplier=1)
            nc.gpsimd.memset(m.v_sb[:, :, :], 1.0)
            for e in range(E):
                nc.gpsimd.memset(m.order[:, :, e], float(E - e))
            for n in range(H // HG):
                pool.wait_ge(head_loaded[n % 2], n // 2 * 16 + 16)
                nc.gpsimd.tensor_copy(m.wv[:, seg(n, HG * DH)].rearrange("p (h d) -> p h d", h=HG), wst[:, n % 2, :, 2 * D:KQV]).then_inc(wv_copied, 1)

        @block.vector
        def _(dve):
            dve.wait_ge(x_loaded, 16 * B)
            for t in range(TILES):
                nc.vector.bn_stats(bn[:, t, :], m.x_sb[:, t, :]).then_inc(dve_chain, 1)
            for t in range(TILES):
                dve.wait_ge(dve_chain, t + 1)
                last = nc.vector.bn_aggr(m.stats[:, t, :], bn[:, t, :])
            last.then_inc(dve_chain, 1)
            dve.wait_ge(dve_chain, TILES + 1)
            c = Chain(dve, dve_chain, 0, TILES + 2 + RSQRT_LINKS)
            c.n = TILES + 1
            c.link(nc.vector.tensor_copy(var[:, :], m.stats[:, :, 1]))
            rsqrt_steps(nc, c.link, var[:, :], m.rstd[:, :], tmp[:, :])
            c.end()
            def turn(t):
                for k in range(4):
                    dve.wait_ge(mh_ready, t * 4 + k + 1)
                    ps = m.psum[2 + k % 2]
                    nc.vector.scalar_tensor_tensor(out=m.ml[:, bass.ds(t * 4 + k, 1), :], in0=ps[:, 0:D], scalar=SCALE, in1=f(m.mh[:, bass.ds(t * 4 + k, 1), :]), op0=ALU.mult, op1=ALU.subtract)
                    nc.vector.tensor_scalar(m.bq[:, bass.ds(t * 4 + k, 1)], ps[:, D:D + 1], SCALE, None, ALU.mult).then_inc(ml_ready, 1)
            loop(dve, H // (2 * HG), turn)

        @block.tensor
        def _(pe):
            pe.wait_ge(ident_made, 2)
            pe.wait_ge(small_loaded, 16 * 6)
            nc.tensor.transpose(m.psum[6][:, 0:H], bias_rows[:, D:2 * D], m.ident[0:H, 0:H])
            nc.tensor.transpose(m.psum[6][:, H:H + E], rw_rows[:, :], m.ident[0:E, 0:E]).then_inc(bias_T, 1)
            pe.wait_ge(bias_copied, 1)
            def turn(t):
                for k in range(4):
                    s, j = k // HG, k % HG
                    if j == 0:
                        pe.wait_ge(head_loaded[s], t * 16 + 16)
                    if positive(t * 4 + k - 1):
                        pe.wait_ge(w_copied, t * 4 + k - 1)
                    for c in range(2):
                        last = nc.tensor.transpose(m.psum[k % 2][:, c * D:(c + 1) * D], wst[:, s, j, c * D:(c + 1) * D], m.ident[:, :])
                    last.then_inc(w_T, 1)
                    pe.wait_ge(w_copied, t * 4 + k + 1)
                    if positive(t * 4 + k - 1):
                        pe.wait_ge(ml_ready, t * 4 + k - 1)
                    nc.tensor.matmul(m.psum[2 + k % 2][:, 0:D], wT[:, k % 2, D:2 * D], wT[:, k % 2, 0:D], start=True, stop=True)
                    nc.tensor.matmul(m.psum[2 + k % 2][:, D:D + 1], wT[:, k % 2, 0:D], bqT[:, bass.ds(t * 4 + k, 1)], start=True, stop=True).then_inc(m_done, 1)
            loop(pe, H // (2 * HG), turn)
            pe.wait_ge(shared_loaded, 48)
            for k in range(6):
                at = k * P
                nc_out = m.psum[4 + at // 512][:, at % 512:at % 512 + P]
                src = sh_rows[:, k // 2, (k % 2) * P:(k % 2) * P + P]
                last = nc.tensor.transpose(nc_out, src, m.ident[:, :])
                if k in (3, 5):
                    last.then_inc(shared_T, 1)


def first_norm(nc, m, ctx):
    sb, sem = tiles(nc, ctx), nc.alloc_semaphore
    xn = sb("xn", [P, 2, TB, D], F32)
    xst = sb("xst", [P, 2, N], F32)
    xn_ready, x_T, xst_ready, xh_ready, xl_ready, v_done, v_ready, xb_done = (
        sem(n) for n in ("xn_ready", "x_T", "xst_ready", "xh_ready", "xl_ready", "v_done", "v_ready", "xb_done"))

    with nc.Block() as block:

        @block.vector
        def _(dve):
            def turn(t):
                for s in range(2):
                    b = t * 2 + s
                    if positive(b - 1):
                        dve.wait_ge(x_T, b - 1)
                    for i in range(TB):
                        last = nc.vector.tensor_scalar(xn[:, s, i, :], m.x_sb[:, bass.ds(b * TB + i, 1), :], m.stats[:, bass.ds(b * TB + i, 1), 0], m.rstd[:, bass.ds(b * TB + i, 1)], ALU.subtract, ALU.mult)
                    last.then_inc(xn_ready, 1)
                for s in range(2):
                    b = t * 2 + s
                    dve.wait_ge(xst_ready, b + 1)
                    dve.wait_ge(xh_ready, b + 1)
                    nc.vector.tensor_tensor(m.xl[:, seg(b, N)], xst[:, s, :], f(m.xh[:, seg(b, N)]), ALU.subtract).then_inc(xl_ready, 1)
                for s in range(2):
                    b = t * 2 + s
                    dve.wait_ge(v_done, b + 1)
                    nc.vector.tensor_tensor(m.v_sb[:, bass.ds(b * TB, TB), :].rearrange("p t (h d) -> p t h d", h=H)[:, :, :, 0:DH],
                                            m.psum[2 + s][:, :].rearrange("p (t h d) -> p t h d", t=TB, h=H),
                                            m.bv_bc[:, :, :].unsqueeze(1).to_broadcast([P, TB, H, DH]), ALU.add).then_inc(v_ready, 1)
            loop(dve, B // 2, turn)

        @block.gpsimd
        def _(pool):
            pool.wait_ge(xn_ready, B)
            nc.gpsimd.tensor_tensor(m.x_sb[:, :, :], m.x_sb[:, :, :], m.bp_bc[:, :].unsqueeze(1).to_broadcast([P, TILES, D]), ALU.add).then_inc(xb_done, 1)
            pool.wait_ge(xb_done, 1)

        @block.scalar
        def _(act):
            def turn(t):
                for s in range(2):
                    b = t * 2 + s
                    act.wait_ge(x_T, b + 1)
                    if positive(b - 1):
                        act.wait_ge(v_done, b - 1)
                    if positive(b - 1):
                        act.wait_ge(xl_ready, b - 1)
                    nc.scalar.activation(xst[:, s, :], m.psum[s][:, :], ACT.Copy).then_inc(xst_ready, 1)
                    nc.scalar.activation(m.xh[:, seg(b, N)], m.psum[s][:, :], ACT.Copy).then_inc(xh_ready, 1)
            loop(act, B // 2, turn)

        @block.tensor
        def _(pe):
            def turn(t):
                for s in range(2):
                    b = t * 2 + s
                    pe.wait_ge(xn_ready, b + 1)
                    if positive(b - 1):
                        pe.wait_ge(xh_ready, b - 1)
                    for i in range(TB):
                        last = nc.tensor.transpose(m.psum[s][:, i * P:(i + 1) * P], xn[:, s, i, :], m.ident[:, :])
                    last.then_inc(x_T, 1)
                for s in range(2):
                    b = t * 2 + s
                    pe.wait_ge(xst_ready, b + 1)
                    if positive(b - 1):
                        pe.wait_ge(v_ready, b - 1)
                    for i in range(TB):
                        last = nc.tensor.matmul(m.psum[2 + s][:, i * P:(i + 1) * P], xst[:, s, i * P:(i + 1) * P], m.wv[:, :], start=True, stop=True)
                    last.then_inc(v_done, 1)
            loop(pe, B // 2, turn)


def attention(nc, m, ctx):
    sb, sem = tiles(nc, ctx), nc.alloc_semaphore
    mst = sb("mst", [P, 2, 2 * D], F32R)
    bst = sb("bst", [P, 2], F32)
    vst = sb("vst", [P, 2, TB, V1], F32)
    qh = [sb(f"qh{k}", [P, N], F32R) for k in range(2)]
    ql = [sb(f"ql{k}", [P, N], F32R) for k in range(2)]
    nmax = sb("nmax", [P, 4], F32)
    p_sb = [sb(f"p_sb{k}", [P, N], F32) for k in range(4)]
    pT_sb = [sb(f"pT_sb{k}", [P, N], F32) for k in range(2)]
    S_BANK, Q_BANK, T_BANK, O_BANK = (0, 1, 2, 3), 4, (5, 6), 7

    m_staged = sem("m_staged")
    v_staged = sem("v_staged")
    q_done = sem("q_done")
    qh_ready = sem("qh_ready")
    ql_ready = sem("ql_ready")
    s_done = sem("s_done")
    max_ready = sem("max_ready")
    exp_done = sem("exp_done")
    t_done = sem("t_done")
    pT_small = sem("pT_small")
    pT_large = sem("pT_large")
    pv_done = sem("pv_done")
    o_ready = sem("o_ready")

    TURNS = B * H // 2
    STEPS = 8 * TURNS

    def turn_slots(turn, emit):
        for s in range(8):
            for stage, lag in (("q", 0), ("s", 2), ("t", 4), ("o", 5)):
                back, r = divmod(s - lag, 8)
                own = turn + back
                if isinstance(own, int) and not 0 <= own < TURNS:
                    continue
                emit(stage, own * 8 + r, own * 2 + r // 4, own, r)

    def run(eng, emit):
        turn_slots(0, emit)
        with eng.Fori(1, TURNS) as turn:
            turn_slots(turn, emit)
        turn_slots(TURNS, emit)


    with nc.Block() as block:

        @block.gpsimd
        def _(pool):
            def pair(turn):
                b = turn // (H // 2)
                hp = turn % (H // 2)
                for k in range(2):
                    h = hp * 2 + k
                    g = turn * 2 + k
                    if positive(g - 1):
                        pool.wait_ge(ql_ready, g - 1)
                    nc.gpsimd.tensor_copy(mst[:, k, 0:D], f(m.mh[:, seg1(h), :]))
                    nc.gpsimd.tensor_copy(mst[:, k, D:2 * D], f(m.ml[:, seg1(h), :]))
                    nc.gpsimd.tensor_copy(bst[:, k:k + 1], m.bq[:, seg1(h)]).then_inc(m_staged, 1)
                    if positive(g * 4 - 4):
                        pool.wait_ge(pv_done, g * 4 - 4)
                    nc.gpsimd.tensor_copy(vst[:, k, :, :], m.v_sb[:, seg(b, TB), seg(h, V1)]).then_inc(v_staged, 1)

            def seg1(i):
                return slice(i, i + 1) if isinstance(i, int) else bass.ds(i, 1)

            pair(0)
            with pool.Fori(1, TURNS) as turn:
                pair(turn)

        @block.tensor
        def _(pe):
            def emit(stage, u, g, turn, r):
                k, i = r // 4, r % 4
                b = turn // (H // 2)
                if stage == "q" and i == 0:
                    pe.wait_ge(m_staged, g + 1)
                    if positive(g):
                        pe.wait_ge(ql_ready, g)
                    x_h, x_l = m.xh[:, seg(b, N)], m.xl[:, seg(b, N)]
                    bank = m.psum[Q_BANK][:, :]
                    nc.tensor.matmul(bank, mst[:, k, 0:D], x_h, start=True, stop=False)
                    nc.tensor.matmul(bank, mst[:, k, 0:D], x_l, start=False, stop=False)
                    nc.tensor.matmul(bank, mst[:, k, D:2 * D], x_h, start=False, stop=True).then_inc(q_done, 1)
                if stage == "s":
                    w = (i + 1) * P
                    if i == 0:
                        pe.wait_ge(ql_ready, g + 1)
                    if positive(u - 3):
                        pe.wait_ge(exp_done, u - 3)
                    x_h, x_l = m.xh[:, seg(b, N, w)], m.xl[:, seg(b, N, w)]
                    q_h, q_l = (q[k][:, i * P:(i + 1) * P] for q in (qh, ql))
                    bank = m.psum[S_BANK[r % 4]]
                    nc.tensor.matmul(bank[:, 0:w], q_h, x_h, start=True, stop=False)
                    nc.tensor.matmul(bank[:, 0:w], q_h, x_l, start=False, stop=False)
                    nc.tensor.matmul(bank[:, i * P:w], m.ident_b[:, :], m.mask_b[:, :], start=False, stop=False)
                    nc.tensor.matmul(bank[:, 0:w], q_l, x_h, start=False, stop=True).then_inc(s_done, 1)
                if stage == "t":
                    pe.wait_ge(exp_done, u + 1)
                    if i >= 2:
                        pe.wait_ge(pT_small, g * 2 + i - 1)
                    elif positive(g * 2 - 1 + i):
                        pe.wait_ge(pT_large, g * 2 - 1 + i)
                    for j in range(i + 1):
                        last = nc.tensor.transpose(m.psum[T_BANK[r % 2]][:, j * P:(j + 1) * P], p_sb[r % 4][:, j * P:(j + 1) * P], m.ident[:, :])
                    last.then_inc(t_done, 1)
                if stage == "o":
                    if i == 0:
                        pe.wait_ge(v_staged, g + 1)
                        if positive(g):
                            pe.wait_ge(o_ready, g)
                    if i < 2:
                        pe.wait_ge(pT_small, g * 2 + i + 1)
                    else:
                        pe.wait_ge(pT_large, g * 2 + i - 1)
                    for j in range(i + 1):
                        last = nc.tensor.matmul(m.psum[O_BANK][:, i * V1:(i + 1) * V1], pT_sb[r % 2][:, j * P:(j + 1) * P], vst[:, k, j, :], start=(j == 0), stop=(j == i))
                    last.then_inc(pv_done, 1)
            run(pe, emit)

        @block.scalar
        def _(act):
            def emit(stage, u, g, turn, r):
                k, i = r // 4, r % 4
                if stage == "q" and i == 0:
                    act.wait_ge(q_done, g + 1)
                    if positive(g * 4 - 4):
                        act.wait_ge(s_done, g * 4 - 4)
                    nc.scalar.activation(qh[k][:, :], m.psum[Q_BANK][:, :], ACT.Identity, bias=bst[:, k:k + 1]).then_inc(qh_ready, 1)
                if stage == "s":
                    w = (i + 1) * P
                    act.wait_ge(max_ready, u + 1)
                    if positive(u - 3):
                        act.wait_ge(t_done, u - 3)
                    nc.scalar.activation(p_sb[r % 4][:, 0:w], m.psum[S_BANK[r % 4]][:, 0:w], ACT.Exp, bias=nmax[:, r % 4:r % 4 + 1]).then_inc(exp_done, 1)
                if stage == "t" and i < 2:
                    act.wait_ge(t_done, u + 1)
                    if positive(u - 1):
                        act.wait_ge(pv_done, u - 1)
                    nc.scalar.activation(pT_sb[r % 2][:, 0:(i + 1) * P], m.psum[T_BANK[r % 2]][:, 0:(i + 1) * P], ACT.Copy).then_inc(pT_small, 1)
            run(act, emit)

        @block.vector
        def _(dve):
            def emit(stage, u, g, turn, r):
                k, i = r // 4, r % 4
                if stage == "q" and i == 0:
                    dve.wait_ge(qh_ready, g + 1)
                    if positive(g * 4 - 4):
                        dve.wait_ge(s_done, g * 4 - 4)
                    nc.vector.scalar_tensor_tensor(out=ql[k][:, :], in0=m.psum[Q_BANK][:, :], scalar=bst[:, k:k + 1], in1=f(qh[k][:, :]), op0=ALU.add, op1=ALU.subtract).then_inc(ql_ready, 1)
                if stage == "s":
                    dve.wait_ge(s_done, u + 1)
                    if positive(u - 3):
                        dve.wait_ge(exp_done, u - 3)
                    nc.vector.tensor_reduce(out=nmax[:, r % 4:r % 4 + 1], in_=m.psum[S_BANK[r % 4]][:, 0:(i + 1) * P], axis=AX.X, op=ALU.max, negate=True).then_inc(max_ready, 1)
                if stage == "t" and i >= 2:
                    dve.wait_ge(t_done, u + 1)
                    if positive(u - 1):
                        dve.wait_ge(pv_done, u - 1)
                    nc.vector.tensor_copy(pT_sb[r % 2][:, 0:(i + 1) * P], m.psum[T_BANK[r % 2]][:, 0:(i + 1) * P]).then_inc(pT_large, 1)
                if stage == "o" and i == 3:
                    b = turn // (H // 2)
                    h = (turn % (H // 2)) * 2 + k
                    dve.wait_ge(pv_done, u + 1)
                    nc.vector.tensor_copy(m.o_sb[:, seg(b, TB), seg(h, V1)], m.psum[O_BANK][:, 0:TB * V1].rearrange("p (t d) -> p t d", t=TB)).then_inc(o_ready, 1)
            run(dve, emit)


def after_attention(nc, m, ctx):
    sb, sem = tiles(nc, ctx), nc.alloc_semaphore
    rinv = sb("rinv", [P, 2, TB, H], F32)
    on = sb("on", [P, 2, TB, D], F32)
    onT = sb("onT", [P, 2, N], F32)
    hn = sb("hn", [P, 2, TB, D], F32)
    hst = sb("hst", [P, 2, N], F32)
    bn = sb("bn2", [P, 2 * TB, 6], F32)
    mv = sb("mv2", [P, 2 * TB, 2], F32)
    var = sb("var2", [P, 2 * TB], F32)
    rstd = sb("rstd2", [P, 2 * TB], F32)
    tmp = sb("tmp2", [P, 2 * TB], F32)
    lg = sb("lg", [P, 2, TB, E], F32)
    ex = sb("ex", [P, 2 * TB, E], F32)
    pr = sb("pr", [P, 2 * TB, E], F32)
    p2 = sb("p2", [P, 2 * TB, E], F32)
    eq = sb("eq", [P, 2 * TB, E], F32)
    sel = sb("sel", [P, 2, 2 * TB, E], F32)
    top = sb("top", [P, 4, 2 * TB], F32)
    w_sb = sb("w_sb", [P, 2 * TB, E], F32)
    wT_sb = sb("wT_sb", [E, 2, N], F32)
    names = ("on_ready", "on_T", "onT_ready", "proj_done", "hn_ready", "h_T", "hst_ready", "hh_ready", "hl_ready",
             "logits_done", "lg_ready", "ex_ready", "w_ready", "w_T2", "wT_ready", "w_stored", "dve_chain3")
    (on_ready, on_T, onT_ready, proj_done, hn_ready, h_T, hst_ready, hh_ready, hl_ready,
     logits_done, lg_ready, ex_ready, w_ready, w_T2, wT_ready, w_stored, dve_chain) = (sem(n) for n in names)

    def bank(kind, s):
        return m.psum[kind * 2 + s]

    with nc.Block() as block:

        @block.vector
        def _(dve):
            def turn(t):
                c = Chain(dve, dve_chain, t, CHAIN3)
                for s in range(2):
                    o = m.o_sb[:, seg(t * 2 + s, TB), :].rearrange("p t (h d) -> p t h d", h=H)
                    c.link(nc.vector.reciprocal(rinv[:, s, :, :], o[:, :, :, DH]))
                for s in range(2):
                    o = m.o_sb[:, seg(t * 2 + s, TB), :].rearrange("p t (h d) -> p t h d", h=H)
                    nc.vector.tensor_tensor(on[:, s, :, :].rearrange("p t (h d) -> p t h d", h=H), o[:, :, :, 0:DH],
                                            rinv[:, s, :, :].unsqueeze(3).to_broadcast([P, TB, H, DH]), ALU.mult).then_inc(on_ready, 1)
                for s in range(2):
                    dve.wait_ge(proj_done, t * 2 + s + 1)
                    xs = m.x_sb[:, seg(t * 2 + s, TB), :]
                    c.link(nc.vector.tensor_tensor(xs, bank(1, s)[:, :].rearrange("p (t d) -> p t d", t=TB), xs, ALU.add))
                if not isinstance(t, int):
                    carry(dve, m)
                for i in range(2 * TB):
                    last = nc.vector.bn_stats(bn[:, i, :], m.x_sb[:, bass.ds(t * 2 * TB + i, 1), :])
                c.link(last)
                if not isinstance(t, int):
                    carry(dve, m)
                for i in range(2 * TB):
                    last = nc.vector.bn_aggr(mv[:, i, :], bn[:, i, :])
                c.link(last)
                c.link(nc.vector.tensor_copy(var[:, :], mv[:, :, 1]))
                rsqrt_steps(nc, c.link, var[:, :], rstd[:, :], tmp[:, :])
                for s in range(2):
                    for i in range(TB):
                        a = s * TB + i
                        last = nc.vector.tensor_scalar(hn[:, s, i, :], m.x_sb[:, bass.ds(t * 2 * TB + a, 1), :], mv[:, a, 0:1], rstd[:, a:a + 1], ALU.subtract, ALU.mult)
                    last.then_inc(hn_ready, 1)
                for s in range(2):
                    dve.wait_ge(hst_ready, t * 2 + s + 1)
                    dve.wait_ge(hh_ready, t * 2 + s + 1)
                    nc.vector.tensor_tensor(m.xl[:, seg(t * 2 + s, N)], hst[:, s, :], f(m.xh[:, seg(t * 2 + s, N)]), ALU.subtract).then_inc(hl_ready, 1)
                for s in range(2):
                    dve.wait_ge(logits_done, t * 2 + s + 1)
                    nc.vector.tensor_tensor(lg[:, s, :, :], bank(2, s)[:, 0:TB * E].rearrange("p (t e) -> p t e", e=E),
                                            m.rb_bc[:, :].unsqueeze(1).to_broadcast([P, TB, E]), ALU.add).then_inc(lg_ready, 1)
                dve.wait_ge(ex_ready, t + 1)
                c.link(nc.vector.tensor_scalar(ex[:, :, :], ex[:, :, :], 1.0, None, ALU.add))
                c.link(nc.vector.reciprocal(pr[:, :, :], ex[:, :, :]))
                src = pr
                for k in range(2):
                    best, first = top[:, 2 * k, :], top[:, 2 * k + 1, :]
                    c.link(nc.vector.tensor_reduce(out=best, in_=src[:, :, :], axis=AX.X, op=ALU.max))
                    c.link(nc.vector.tensor_tensor(eq[:, :, :], src[:, :, :], best.unsqueeze(2).to_broadcast([P, 2 * TB, E]), ALU.is_equal))
                    c.link(nc.vector.tensor_tensor(eq[:, :, :], eq[:, :, :], m.order[:, :, :], ALU.mult))
                    c.link(nc.vector.tensor_reduce(out=first, in_=eq[:, :, :], axis=AX.X, op=ALU.max))
                    c.link(nc.vector.tensor_tensor(sel[:, k, :, :], m.order[:, :, :], first.unsqueeze(2).to_broadcast([P, 2 * TB, E]), ALU.is_equal))
                    if k == 0:
                        c.link(nc.vector.scalar_tensor_tensor(out=p2[:, :, :], in0=sel[:, 0, :, :], scalar=-2.0, in1=pr[:, :, :], op0=ALU.mult, op1=ALU.add))
                        src = p2
                c.link(nc.vector.tensor_tensor(eq[:, :, :], sel[:, 0, :, :], sel[:, 1, :, :], ALU.add))
                c.link(nc.vector.tensor_tensor(eq[:, :, :], eq[:, :, :], pr[:, :, :], ALU.mult))
                c.link(nc.vector.tensor_tensor(top[:, 1, :], top[:, 0, :], top[:, 2, :], ALU.add))
                c.link(nc.vector.reciprocal(top[:, 3, :], top[:, 1, :]))
                nc.vector.tensor_tensor(w_sb[:, :, :], eq[:, :, :], top[:, 3, :].unsqueeze(2).to_broadcast([P, 2 * TB, E]), ALU.mult).then_inc(w_ready, 1)
                c.end()
            loop(dve, B // 2, turn)

        @block.tensor
        def _(pe):
            def turn(t):
                for s in range(2):
                    pe.wait_ge(on_ready, t * 2 + s + 1)
                    for i in range(TB):
                        last = nc.tensor.transpose(bank(0, s)[:, i * P:(i + 1) * P], on[:, s, i, :], m.ident[:, :])
                    last.then_inc(on_T, 1)
                for s in range(2):
                    pe.wait_ge(onT_ready, t * 2 + s + 1)
                    for i in range(TB):
                        last = nc.tensor.matmul(bank(1, s)[:, i * P:(i + 1) * P], onT[:, s, i * P:(i + 1) * P], m.wp[:, :], start=True, stop=True)
                    last.then_inc(proj_done, 1)
                for s in range(2):
                    pe.wait_ge(hn_ready, t * 2 + s + 1)
                    for i in range(TB):
                        last = nc.tensor.transpose(bank(0, s)[:, i * P:(i + 1) * P], hn[:, s, i, :], m.ident[:, :])
                    last.then_inc(h_T, 1)
                for s in range(2):
                    pe.wait_ge(hst_ready, t * 2 + s + 1)
                    for i in range(TB):
                        last = nc.tensor.matmul(bank(2, s)[:, i * E:(i + 1) * E], hst[:, s, i * P:(i + 1) * P], m.rwT[:, :], start=True, stop=True)
                    last.then_inc(logits_done, 1)
                pe.wait_ge(w_ready, t + 1)
                for s in range(2):
                    if positive(t * 2):
                        pe.wait_ge(wT_ready, t * 2)
                    for i in range(TB):
                        last = nc.tensor.transpose(bank(3, s)[0:E, i * P:(i + 1) * P], w_sb[:, s * TB + i, :], m.ident[:, :])
                    last.then_inc(w_T2, 1)
            loop(pe, B // 2, turn)

        @block.scalar
        def _(act):
            def turn(t):
                for s in range(2):
                    act.wait_ge(on_T, t * 2 + s + 1)
                    nc.scalar.activation(onT[:, s, :], bank(0, s)[:, :], ACT.Copy).then_inc(onT_ready, 1)
                for s in range(2):
                    act.wait_ge(h_T, t * 2 + s + 1)
                    if positive(t * 2):
                        act.wait_ge(hl_ready, t * 2)
                    nc.scalar.activation(hst[:, s, :], bank(0, s)[:, :], ACT.Copy).then_inc(hst_ready, 1)
                    nc.scalar.activation(m.xh[:, seg(t * 2 + s, N)], bank(0, s)[:, :], ACT.Copy).then_inc(hh_ready, 1)
                act.wait_ge(lg_ready, t * 2 + 2)
                nc.scalar.activation(ex[:, :, :], lg[:, :, :, :].rearrange("p s t e -> p (s t) e"), ACT.Exp, scale=-1.0).then_inc(ex_ready, 1)
                for s in range(2):
                    act.wait_ge(w_T2, t * 2 + s + 1)
                    if positive(t * 32):
                        act.wait_ge(w_stored, t * 32)
                    nc.scalar.activation(wT_sb[:, s, :], bank(3, s)[0:E, :], ACT.Copy).then_inc(wT_ready, 1)
            loop(act, B // 2, turn)

        @block.sync
        def _(sp):
            def turn(t):
                for s in range(2):
                    sp.wait_ge(wT_ready, t * 2 + s + 1)
                    sp.dma_start(m.w_dram[:, seg(t * 2 + s, N)], wT_sb[:, s, :]).then_inc(w_stored, 16)
            loop(sp, B // 2, turn)
            sp.wait_ge(w_stored, 16 * B)


CHAIN3 = 2 + 2 + 1 + 1 + 1 + RSQRT_LINKS + 2 + 11 + 4


def experts(nc, m, ctx):
    sb, sem = tiles(nc, ctx), nc.alloc_semaphore
    wbc = [sb(f"wbc{s}", [P, TOK], F32) for s in range(2)]
    y = m.v_sb[:, :, :].rearrange("p t c -> p (t c)")[:, 0:TOK]
    sg = sb("sg", [P, 2, N], F32)
    su = sb("su", [P, 2, N], F32)
    gu = [sb(f"gu{s}", [P, 2, N], F32) for s in range(2)]
    guh = [[sb(f"guh{s}{k}", [P, N], F32R) for k in range(2)] for s in range(2)]
    gul = [[sb(f"gul{s}{k}", [P, N], F32R) for k in range(2)] for s in range(2)]
    yst = sb("yst", [P, 2, N], F32)
    out_sb = sb("out_sb", [P, 2, TB, D], F32)
    w_loaded = [sem(f"w_loaded{s}") for s in range(2)]
    wbc_loaded = [sem(f"wbc_loaded{s}") for s in range(2)]
    wh_ready = sem("wh_ready")
    w_split = sem("w_split")
    ones_made = sem("ones_made")
    y_zero = sem("y_zero")
    gate_up = sem("gate_up")
    silu_ready = sem("silu_ready")
    su_ready = sem("su_ready")
    gu_ready = sem("gu_ready")
    guh_ready = sem("guh_ready")
    gul_ready = sem("gul_ready")
    down_done = sem("down_done")
    y_added = sem("y_added")
    yst_ready, y_T, out_ready, out_stored = (sem(n) for n in ("yst_ready", "y_T", "out_ready", "out_stored"))
    GB, UB, YB = (0, 1), (2, 3), 4
    BATCHES = (E + 1) * B


    def sweep(eng, one, between=None):
        def expert(p, slot):
            for par in range(2):
                one(p, slot, 0 + par, par)
            if between:
                between(p, slot)
            with eng.Fori(1, B // 2) as j:
                for par in range(2):
                    one(p, slot, j * 2 + par, par)
        expert(0, 0)
        with eng.Fori(0, E // 2) as q:
            expert(q * 2 + 1, 1)
            expert(q * 2 + 2, 0)

    with nc.Block() as block:

        @block.sync
        def _(sp):
            def load(e, p, slot):
                if positive(p - 1):
                    sp.wait_ge(w_split, p - 1)
                ei = slice(e, e + 1) if isinstance(e, int) else bass.ds(e, 1)
                sp.dma_start(m.wraw[:, slot, 0:I], m.gate_w[ei, :, :].rearrange("e h i -> h (e i)")).then_inc(w_loaded[slot], 16)
                sp.dma_start(m.wraw[:, slot, I:2 * I], m.up_w[ei, :, :].rearrange("e h i -> h (e i)")).then_inc(w_loaded[slot], 16)
                sp.dma_start(m.wraw[:, slot, 2 * I:EW].rearrange("p (k d) -> p k d", k=2), m.down_w[ei, :, :].rearrange("e (k p) d -> p (e k) d", p=P)).then_inc(w_loaded[slot], 16)
                if positive((p - 1) * 2 * B):
                    sp.wait_ge(gu_ready, (p - 1) * 2 * B)
                sp.dma_start(wbc[slot][:, :], m.w_dram[ei, :].rearrange("e t -> (e t)").partition_broadcast(P)).then_inc(wbc_loaded[slot], 16)
            load(0, 1, 1)
            load(1, 2, 0)
            with sp.Fori(1, E // 2) as q:
                load(q * 2, q * 2 + 1, 1)
                load(q * 2 + 1, q * 2 + 2, 0)
            def turn(t):
                for s in range(2):
                    sp.wait_ge(out_ready, t * 2 + s + 1)
                    sp.dma_start(m.out[bass.ds(t * 2 + s, 1), :, :].rearrange("b (t p) d -> p (b t) d", p=P), out_sb[:, s, :, :]).then_inc(out_stored, 16)
            loop(sp, B // 2, turn)
            sp.wait_ge(out_stored, 16 * B)

        @block.gpsimd
        def _(pool):
            def split(p, slot):
                if positive(p):
                    if positive((p - 1) * B):
                        pool.wait_ge(down_done, (p - 1) * B)
                    pool.wait_ge(w_loaded[slot], ((p - 1) // 2) * 48 + 48)
                nc.gpsimd.tensor_tensor(m.wh[slot][:, :], m.wraw[:, slot, :], m.carrier[:, 0:1].to_broadcast([P, EW]), ALU.add).then_inc(wh_ready, 1)
                pool.wait_ge(wh_ready, p + 1)
                nc.gpsimd.tensor_tensor(m.wl[slot][:, :], m.wraw[:, slot, :], f(m.wh[slot][:, :]), ALU.subtract).then_inc(w_split, 1)

            def one(p, slot, b, par):
                nb = p * B + b
                for k in range(2):
                    pool.wait_ge(guh_ready, nb * 2 + k + 1)
                    if positive(nb - 1):
                        pool.wait_ge(down_done, nb - 1)
                    nc.gpsimd.tensor_tensor(gul[par][k][:, :], gu[par][:, k, :], f(guh[par][k][:, :]), ALU.subtract).then_inc(gul_ready, 1)

            nc.gpsimd.memset(wbc[0][:, :], 1.0).then_inc(ones_made, 1)
            pool.wait_ge(ones_made, 1)
            nc.gpsimd.memset(y, 0.0).then_inc(y_zero, 1)
            split(0, 0)
            def expert(p, slot, last=False):
                for par in range(2):
                    one(p, slot, par, par)
                if not last:
                    split(p + 1, 1 - slot)
                with pool.Fori(1, B // 2) as j:
                    for par in range(2):
                        one(p, slot, j * 2 + par, par)
            expert(0, 0)
            with pool.Fori(0, E // 2 - 1) as q:
                expert(q * 2 + 1, 1)
                expert(q * 2 + 2, 0)
            expert(E - 1, 1)
            expert(E, 0, last=True)

        @block.tensor
        def _(pe):
            def down(slot, n_batch, par):
                if positive(n_batch):
                    pe.wait_ge(y_added, n_batch)
                for k in range(2):
                    pe.wait_ge(gul_ready, n_batch * 2 + k + 1)
                    w_h = m.wh[slot][:, 2 * I + k * D:2 * I + (k + 1) * D]
                    w_l = m.wl[slot][:, 2 * I + k * D:2 * I + (k + 1) * D]
                    nc.tensor.matmul(m.psum[YB][:, :], w_h, guh[par][k][:, :], start=(k == 0), stop=False)
                    nc.tensor.matmul(m.psum[YB][:, :], w_h, gul[par][k][:, :], start=False, stop=False)
                    last = nc.tensor.matmul(m.psum[YB][:, :], w_l, guh[par][k][:, :], start=False, stop=(k == 1))
                last.then_inc(down_done, 1)

            def one(p, slot, b, par):
                nb = p * B + b
                if isinstance(b, int) and b == 0:
                    pe.wait_ge(w_split, p + 1)
                x_h, x_l = m.xh[:, seg(b, N)], m.xl[:, seg(b, N)]
                for k in range(2):
                    if positive(nb * 2 + k - 1):
                        pe.wait_ge(su_ready, nb * 2 + k - 1)
                    for c, banks in ((0, GB), (1, UB)):
                        w_h = m.wh[slot][:, c * I + k * P:c * I + (k + 1) * P]
                        w_l = m.wl[slot][:, c * I + k * P:c * I + (k + 1) * P]
                        bank = m.psum[banks[k]][:, :]
                        nc.tensor.matmul(bank, w_h, x_h, start=True, stop=False)
                        nc.tensor.matmul(bank, w_h, x_l, start=False, stop=False)
                        last = nc.tensor.matmul(bank, w_l, x_h, start=False, stop=True)
                    last.then_inc(gate_up, 1)
                if isinstance(b, int) and b == 0:
                    if positive(p):
                        down(1 - slot, nb - 1, 1)
                else:
                    down(slot, nb - 1, 1 - par)
            sweep(pe, one)
            down(0, BATCHES - 1, 1)
            def turn(t):
                for s in range(2):
                    pe.wait_ge(yst_ready, t * 2 + s + 1)
                    if positive(t * 2):
                        pe.wait_ge(out_ready, t * 2)
                    for i in range(TB):
                        last = nc.tensor.transpose(m.psum[5 + s][:, i * P:(i + 1) * P], yst[:, s, i * P:(i + 1) * P], m.ident[:, :])
                    last.then_inc(y_T, 1)
            loop(pe, B // 2, turn)

        @block.scalar
        def _(act):
            def one(p, slot, b, par):
                nb = p * B + b
                for k in range(2):
                    n = nb * 2 + k
                    act.wait_ge(gate_up, n + 1)
                    if positive(n - 1):
                        act.wait_ge(su_ready, n - 1)
                    nc.scalar.activation(sg[:, k, :], m.psum[GB[k]][:, :], ACT.Silu).then_inc(silu_ready, 1)
                for k in range(2):
                    n = nb * 2 + k
                    act.wait_ge(gu_ready, n + 1)
                    if positive(nb - 1):
                        act.wait_ge(down_done, nb - 1)
                    nc.scalar.activation(guh[par][k][:, :], gu[par][:, k, :], ACT.Copy).then_inc(guh_ready, 1)
            sweep(act, one)
            def turn(t):
                for s in range(2):
                    act.wait_ge(y_added, BATCHES)
                    if positive(t * 2):
                        act.wait_ge(y_T, t * 2)
                    nc.scalar.activation(yst[:, s, :], y[:, seg(t * 2 + s, N)], ACT.Copy).then_inc(yst_ready, 1)
            loop(act, B // 2, turn)

        @block.vector
        def _(dve):
            def add_y(nb, b):
                dve.wait_ge(down_done, nb + 1)
                if isinstance(nb, int) and nb == 0:
                    dve.wait_ge(y_zero, 1)
                ys = y[:, seg(b, N)]
                nc.vector.tensor_tensor(ys, m.psum[YB][:, :], ys, ALU.add).then_inc(y_added, 1)

            def one(p, slot, b, par):
                nb = p * B + b
                if isinstance(b, int) and b == 0:
                    if isinstance(p, int) and p == 0:
                        dve.wait_ge(ones_made, 1)
                    else:
                        dve.wait_ge(wbc_loaded[slot], ((p - 1) // 2) * 16 + 16)
                for k in range(2):
                    n = nb * 2 + k
                    dve.wait_ge(silu_ready, n + 1)
                    if positive(n - 1):
                        dve.wait_ge(gu_ready, n - 1)
                    nc.vector.tensor_tensor(su[:, k, :], m.psum[UB[k]][:, :], sg[:, k, :], ALU.mult).then_inc(su_ready, 1)
                for k in range(2):
                    n = nb * 2 + k
                    dve.wait_ge(su_ready, n + 1)
                    if positive(n - 3):
                        dve.wait_ge(gul_ready, n - 3)
                    nc.vector.tensor_tensor(gu[par][:, k, :], su[:, k, :], wbc[slot][:, seg(b, N)], ALU.mult).then_inc(gu_ready, 1)
                if isinstance(b, int) and b == 0:
                    if positive(p):
                        add_y(nb - 1, B - 1)
                else:
                    add_y(nb - 1, b - 1)
            sweep(dve, one)
            add_y(BATCHES - 1, B - 1)
            def turn(t):
                for s in range(2):
                    dve.wait_ge(y_T, t * 2 + s + 1)
                    if positive(t * 32):
                        dve.wait_ge(out_stored, t * 32)
                    nc.vector.tensor_tensor(out_sb[:, s, :, :], m.psum[5 + s][:, :].rearrange("p (t d) -> p t d", t=TB), m.x_sb[:, seg(t * 2 + s, TB), :], ALU.add).then_inc(out_ready, 1)
            loop(dve, B // 2, turn)


def layer(nc, io):
    m = Mem(nc, io)
    for phase in (prepare, first_norm, attention, after_attention, experts):
        with ExitStack() as ctx:
            phase(nc, m, ctx)


_INS = {"L0_attn_x": "x", "L0_attn_Wkqv": "Wkqv", "L0_attn_bkqv": "bkqv", "L0_attn_Wp": "Wp", "L0_attn_bp": "bp",
        "L0_ffn_shared_gate": "shared_gate", "L0_ffn_shared_up": "shared_up", "L0_ffn_shared_down": "shared_down",
        "L0_ffn_gate_w": "gate_w", "L0_ffn_up_w": "up_w", "L0_ffn_down_w": "down_w",
        "L0_ffn_router_w": "router_w", "L0_ffn_routing_bias": "routing_bias"}


def kernel(**inputs):
    import concourse.bacc as bacc
    from concourse.bass_utils import run_bass_kernel_spmd as run

    nc = bacc.Bacc("TRN2", target_bir_lowering=False, num_devices=1)
    arrays, io = {}, []
    for name, short in _INS.items():
        a = np.ascontiguousarray(inputs[name])
        arrays[f"in_{short}"] = a
        io.append(nc.dram_tensor(f"in_{short}", a.shape, mybir.dt.from_np(a.dtype), kind="ExternalInput").ap())
    io.append(nc.dram_tensor("out", (B, N, D), F32, kind="ExternalOutput").ap())
    io.append(nc.dram_tensor("w_dram", (E, TOK), F32, kind="Internal").ap())
    layer(nc, io)
    r = run(nc, [arrays], core_ids=[0])
    return r.results[0]["out"]
```

```python
import concourse.bass as bass
from concourse import mybir
import numpy as np
from contextlib import ExitStack

F32 = mybir.dt.float32
F32R = mybir.dt.float32r
BF16 = mybir.dt.bfloat16
F16 = mybir.dt.float16
I32 = mybir.dt.int32
ALU = mybir.AluOpType
ACT = mybir.ActivationFunctionType
AX = mybir.AxisListType

P = 128
B, N, D = 8, 512, 128
H, DH = 16, 8
E, I = 8, 256
TB = N // P
TOK = B * N
TILES = B * TB
KQV = 2 * D + DH
V1 = DH + 1
PARTS = 3
VC = V1 * PARTS
LIFT = 32768.0
EW = 2 * I + 2 * D
SCALE = float(D) ** -0.5
EPS = 1e-5
MASKED = -1e30
RSQRT_MAGIC = float(0x5F3759DF)


def f(ap):
    return ap.bitcast(F32)


def seg(i, n, width=None):
    width = n if width is None else width
    return slice(i * n, i * n + width) if isinstance(i, int) else bass.ds(i * n, width)


def one_of(i):
    return slice(i, i + 1) if isinstance(i, int) else bass.ds(i, 1)


def tiles(nc, ctx):
    return lambda name, shape, dtype: ctx.enter_context(nc.sbuf_tensor(name, shape, dtype))


def positive(value):
    return not isinstance(value, int) or value > 0


def carry(eng, m):
    m.carriers += 1
    eng.memset(m.carrier[:, m.carriers:m.carriers + 1], 0.0)


def loop(eng, turns, body):
    body(0)
    with eng.Fori(1, turns) as t:
        body(t)


class Chain:

    def __init__(self, eng, sem, turn, per):
        self.eng, self.sem, self.base, self.n, self.per = eng, sem, turn * per, 0, per

    def link(self, ins):
        ins.then_inc(self.sem, 1)
        self.n += 1
        self.eng.wait_ge(self.sem, self.base + self.n)

    def end(self):
        assert self.n == self.per, (self.n, self.per)


def rsqrt_steps(nc, link, v, y, t):
    link(nc.vector.tensor_scalar(v, v, EPS, None, ALU.add))
    link(nc.vector.tensor_scalar(t.bitcast(I32), v.bitcast(I32), 1, None, ALU.logical_shift_right))
    link(nc.vector.tensor_scalar(y.bitcast(I32), t.bitcast(I32), -1.0, RSQRT_MAGIC, ALU.mult, ALU.add))
    for _ in range(4):
        link(nc.vector.tensor_tensor(t, y, y, ALU.mult))
        link(nc.vector.tensor_tensor(t, t, v, ALU.mult))
        link(nc.vector.tensor_scalar(t, t, -0.5, 1.5, ALU.mult, ALU.add))
        link(nc.vector.tensor_tensor(y, y, t, ALU.mult))


RSQRT_LINKS = 3 + 4 * 4


class Mem:

    def __init__(self, nc, io):
        (self.x, self.Wkqv, self.bkqv, self.Wp, self.bp, self.shared_gate, self.shared_up, self.shared_down, self.gate_w,
         self.up_w, self.down_w, self.router_w, self.routing_bias, self.out, self.w_dram) = io
        sb = nc.alloc_sbuf_tensor
        self.carrier = sb("carrier", [P, 64], F32)
        self.carriers = 0
        self.ident = sb("ident", [P, P], F32)
        self.ident_b = sb("ident_b", [P, P], BF16)
        self.mask_b = sb("mask_b", [P, P], BF16)
        self.bv_bc = sb("bv_bc", [P, H, DH], F32)
        self.bp_bc = sb("bp_bc", [P, D], F32)
        self.rb_bc = sb("rb_bc", [P, E], F32)
        self.order = sb("order", [P, 2 * TB, E], F32)
        self.x_sb = sb("x_sb", [P, TILES, D], F32)
        self.xh = sb("xh", [P, TOK], F32R)
        self.xl = sb("xl", [P, TOK], F32R)
        self.v_sb = sb("v_sb", [P, TILES, H * VC], BF16)
        self.stats = sb("stats", [P, TILES, 2], F32)
        self.rstd = sb("rstd", [P, TILES], F32)
        self.mh = sb("mh", [P, H, D], F32R)
        self.ml = sb("ml", [P, H, D], F32R)
        self.bq = sb("bq", [P, H], F32)
        self.wv = sb("wv", [P, H * DH], F32)
        self.wp = sb("wp", [P, D], F32)
        self.rwT = sb("rwT", [P, E], F32)
        self.wraw = sb("wraw", [P, 2, EW], F32)
        self.wh = [sb(f"wh{s}", [P, EW], F32R) for s in range(2)]
        self.wl = [sb(f"wl{s}", [P, EW], F32R) for s in range(2)]
        self.psum = [nc.alloc_psum_tensor(f"bank{i}", [P, 512], F32) for i in range(8)]
        self.o_sb = sb("o_sb", [P, TILES, H * V1], F32)


def prepare(nc, m, ctx):
    sb, sem = tiles(nc, ctx), nc.alloc_semaphore
    HG = 2
    wst = sb("wst", [P, 2, HG, KQV], F32)
    wT = sb("wT", [P, 2, 2 * D], F32)
    bias_rows = sb("bias_rows", [H, KQV], F32)
    bqT = sb("bqT", [P, H], F32)
    rw_rows = sb("rw_rows", [E, D], F32)
    sh_rows = sb("sh_rows", [P, 3, I], F32)
    bn = sb("bn", [P, TILES, 6], F32)
    tmp = sb("tmp_rstd", [P, TILES], F32)
    var = sb("var", [P, TILES], F32)

    x_loaded = sem("x_loaded")
    small_loaded = sem("small_loaded")
    shared_loaded = sem("shared_loaded")
    head_loaded = [sem(f"head_loaded{s}") for s in range(2)]
    ident_made = sem("ident_made")
    consts = sem("consts")
    wv_copied = sem("wv_copied")
    bias_T = sem("bias_T")
    bias_copied = sem("bias_copied")
    w_T = sem("w_T")
    w_copied = sem("w_copied")
    m_done = sem("m_done")
    mh_ready = sem("mh_ready")
    ml_ready = sem("ml_ready")
    shared_T = sem("shared_T")
    shared_copied = sem("shared_copied")
    dve_chain = sem("dve_chain0")

    with nc.Block() as block:

        @block.sync
        def _(sp):
            sp.dma_start(bias_rows[:, :], m.bkqv).then_inc(small_loaded, 16)
            sp.dma_start(rw_rows[:, :], m.router_w).then_inc(small_loaded, 16)
            sp.dma_start(m.bv_bc[:, :, :], m.bkqv[:, 2 * D:KQV].partition_broadcast(P)).then_inc(small_loaded, 16)
            sp.dma_start(m.bp_bc[:, :], m.bp.partition_broadcast(P)).then_inc(small_loaded, 16)
            sp.dma_start(m.rb_bc[:, :], m.routing_bias.partition_broadcast(P)).then_inc(small_loaded, 16)
            sp.dma_start(m.wp[:, :], m.Wp).then_inc(small_loaded, 16)
            for n in range(H // HG):
                if n >= 2:
                    sp.wait_ge(m_done, (n - 1) * HG)
                    sp.wait_ge(wv_copied, n - 1)
                sp.dma_start(wst[:, n % 2, :, :], m.Wkqv[n * HG:(n + 1) * HG, :, :].rearrange("h d e -> d h e")).then_inc(head_loaded[n % 2], 16)
            sp.wait_ge(small_loaded, 16 * 6)

        @block.scalar
        def _(act):
            with act.Fori(0, B) as b:
                act.dma_start(m.x_sb[:, bass.ds(b * TB, TB), :], m.x[bass.ds(b, 1), :, :].rearrange("b (t p) d -> p (b t) d", p=P)).then_inc(x_loaded, 16)
            for k in range(2):
                act.dma_start(sh_rows[:, k, :].rearrange("p (t d) -> p t d", t=2), (m.shared_gate, m.shared_up)[k].rearrange("(t p) d -> p t d", p=P)).then_inc(shared_loaded, 16)
            act.dma_start(sh_rows[:, 2, :], m.shared_down).then_inc(shared_loaded, 16)
            act.wait_ge(bias_T, 1)
            nc.scalar.activation(bqT[:, :], m.psum[6][:, 0:H], ACT.Copy)
            nc.scalar.activation(m.rwT[:, :], m.psum[6][:, H:H + E], ACT.Copy).then_inc(bias_copied, 1)
            def turn(t):
                for k in range(4):
                    act.wait_ge(w_T, t * 4 + k + 1)
                    if positive(t * 4 + k - 1):
                        act.wait_ge(m_done, t * 4 + k - 1)
                    nc.scalar.activation(wT[:, k % 2, :], m.psum[k % 2][:, 0:2 * D], ACT.Copy).then_inc(w_copied, 1)
                    act.wait_ge(m_done, t * 4 + k + 1)
                    nc.scalar.activation(m.mh[:, bass.ds(t * 4 + k, 1), :], m.psum[2 + k % 2][:, 0:D], ACT.Copy, scale=SCALE).then_inc(mh_ready, 1)
            loop(act, H // (2 * HG), turn)
            for k in range(2):
                act.wait_ge(shared_T, k + 1)
                nc.scalar.activation(m.wraw[:, 0, k * 512:min(EW, k * 512 + 512)], m.psum[4 + k][:, 0:min(512, EW - k * 512)], ACT.Copy).then_inc(shared_copied, 1)
            act.wait_ge(x_loaded, 16 * B)

        @block.gpsimd
        def _(pool):
            nc.gpsimd.memset(m.carrier[:, 0:1], 0.0)
            nc.gpsimd.memset(m.ident[:, :], 0.0).then_inc(consts, 1)
            nc.gpsimd.memset(m.ident_b[:, :], 0.0).then_inc(consts, 1)
            nc.gpsimd.memset(m.mask_b[:, :], 0.0).then_inc(consts, 1)
            pool.wait_ge(consts, 3)
            for t in (m.ident, m.ident_b):
                nc.gpsimd.affine_select(out=t[:, :], in_=t[:, :], compare_op=ALU.not_equal, fill=1.0, base=0, pattern=[[-1, P]], channel_multiplier=1).then_inc(ident_made, 1)
            nc.gpsimd.affine_select(out=m.mask_b[:, :], in_=m.mask_b[:, :], compare_op=ALU.is_ge, fill=MASKED, base=0, pattern=[[-1, P]], channel_multiplier=1)
            nc.gpsimd.memset(m.v_sb[:, :, :], 0.0).then_inc(consts, 1)
            pool.wait_ge(consts, 4)
            nc.gpsimd.memset(m.v_sb[:, :, :].rearrange("p t (h c k) -> p (t h) c k", c=V1, k=PARTS)[:, :, DH, 0], 1.0)
            for e in range(E):
                nc.gpsimd.memset(m.order[:, :, e], float(E - e))
            for n in range(H // HG):
                pool.wait_ge(head_loaded[n % 2], n // 2 * 16 + 16)
                nc.gpsimd.tensor_copy(m.wv[:, seg(n, HG * DH)].rearrange("p (h d) -> p h d", h=HG), wst[:, n % 2, :, 2 * D:KQV]).then_inc(wv_copied, 1)

        @block.vector
        def _(dve):
            dve.wait_ge(x_loaded, 16 * B)
            for t in range(TILES):
                nc.vector.bn_stats(bn[:, t, :], m.x_sb[:, t, :]).then_inc(dve_chain, 1)
            for t in range(TILES):
                dve.wait_ge(dve_chain, t + 1)
                last = nc.vector.bn_aggr(m.stats[:, t, :], bn[:, t, :])
            last.then_inc(dve_chain, 1)
            dve.wait_ge(dve_chain, TILES + 1)
            c = Chain(dve, dve_chain, 0, TILES + 2 + RSQRT_LINKS)
            c.n = TILES + 1
            c.link(nc.vector.tensor_copy(var[:, :], m.stats[:, :, 1]))
            rsqrt_steps(nc, c.link, var[:, :], m.rstd[:, :], tmp[:, :])
            c.end()
            def turn(t):
                for k in range(4):
                    dve.wait_ge(mh_ready, t * 4 + k + 1)
                    ps = m.psum[2 + k % 2]
                    nc.vector.scalar_tensor_tensor(out=m.ml[:, bass.ds(t * 4 + k, 1), :], in0=ps[:, 0:D], scalar=SCALE, in1=f(m.mh[:, bass.ds(t * 4 + k, 1), :]), op0=ALU.mult, op1=ALU.subtract)
                    nc.vector.tensor_scalar(m.bq[:, bass.ds(t * 4 + k, 1)], ps[:, D:D + 1], SCALE, None, ALU.mult).then_inc(ml_ready, 1)
            loop(dve, H // (2 * HG), turn)

        @block.tensor
        def _(pe):
            pe.wait_ge(ident_made, 2)
            pe.wait_ge(small_loaded, 16 * 6)
            nc.tensor.transpose(m.psum[6][:, 0:H], bias_rows[:, D:2 * D], m.ident[0:H, 0:H])
            nc.tensor.transpose(m.psum[6][:, H:H + E], rw_rows[:, :], m.ident[0:E, 0:E]).then_inc(bias_T, 1)
            pe.wait_ge(bias_copied, 1)
            def turn(t):
                for k in range(4):
                    s, j = k // HG, k % HG
                    if j == 0:
                        pe.wait_ge(head_loaded[s], t * 16 + 16)
                    if positive(t * 4 + k - 1):
                        pe.wait_ge(w_copied, t * 4 + k - 1)
                    for c in range(2):
                        last = nc.tensor.transpose(m.psum[k % 2][:, c * D:(c + 1) * D], wst[:, s, j, c * D:(c + 1) * D], m.ident[:, :])
                    last.then_inc(w_T, 1)
                    pe.wait_ge(w_copied, t * 4 + k + 1)
                    if positive(t * 4 + k - 1):
                        pe.wait_ge(ml_ready, t * 4 + k - 1)
                    nc.tensor.matmul(m.psum[2 + k % 2][:, 0:D], wT[:, k % 2, D:2 * D], wT[:, k % 2, 0:D], start=True, stop=True)
                    nc.tensor.matmul(m.psum[2 + k % 2][:, D:D + 1], wT[:, k % 2, 0:D], bqT[:, bass.ds(t * 4 + k, 1)], start=True, stop=True).then_inc(m_done, 1)
            loop(pe, H // (2 * HG), turn)
            pe.wait_ge(shared_loaded, 48)
            for k in range(6):
                at = k * P
                nc_out = m.psum[4 + at // 512][:, at % 512:at % 512 + P]
                src = sh_rows[:, k // 2, (k % 2) * P:(k % 2) * P + P]
                last = nc.tensor.transpose(nc_out, src, m.ident[:, :])
                if k in (3, 5):
                    last.then_inc(shared_T, 1)


def first_norm(nc, m, ctx):
    sb, sem = tiles(nc, ctx), nc.alloc_semaphore
    xn = sb("xn", [P, 2, TB, D], F32)
    xst = sb("xst", [P, 2, N], F32)
    v32 = sb("v32", [P, TB, H, DH], F32)
    dve_chain = sem("dve_chain1")
    xn_ready, x_T, xst_ready, xh_ready, xl_ready, v_done, v_ready, xb_done = (
        sem(n) for n in ("xn_ready", "x_T", "xst_ready", "xh_ready", "xl_ready", "v_done", "v_ready", "xb_done"))

    with nc.Block() as block:

        @block.vector
        def _(dve):
            def turn(t):
                c = Chain(dve, dve_chain, t, 2 * (2 * PARTS - 1))
                for s in range(2):
                    b = t * 2 + s
                    if positive(b - 1):
                        dve.wait_ge(x_T, b - 1)
                    for i in range(TB):
                        last = nc.vector.tensor_scalar(xn[:, s, i, :], m.x_sb[:, bass.ds(b * TB + i, 1), :], m.stats[:, bass.ds(b * TB + i, 1), 0], m.rstd[:, bass.ds(b * TB + i, 1)], ALU.subtract, ALU.mult)
                    last.then_inc(xn_ready, 1)
                for s in range(2):
                    b = t * 2 + s
                    dve.wait_ge(xst_ready, b + 1)
                    dve.wait_ge(xh_ready, b + 1)
                    nc.vector.tensor_tensor(m.xl[:, seg(b, N)], xst[:, s, :], f(m.xh[:, seg(b, N)]), ALU.subtract).then_inc(xl_ready, 1)
                for s in range(2):
                    b = t * 2 + s
                    dve.wait_ge(v_done, b + 1)
                    c.link(nc.vector.tensor_tensor(v32[:, :, :, :], m.psum[2 + s][:, :].rearrange("p (t h d) -> p t h d", t=TB, h=H),
                                                   m.bv_bc[:, :, :].unsqueeze(1).to_broadcast([P, TB, H, DH]), ALU.add))
                    parts = m.v_sb[:, seg(b, TB), :].rearrange("p t (h c k) -> p t h c k", h=H, c=V1)[:, :, :, 0:DH, :]
                    for k in range(PARTS - 1):
                        c.link(nc.vector.tensor_copy(parts[:, :, :, :, k], v32[:, :, :, :]))
                        c.link(nc.vector.tensor_tensor(v32[:, :, :, :], v32[:, :, :, :], parts[:, :, :, :, k], ALU.subtract))
                    nc.vector.tensor_copy(parts[:, :, :, :, PARTS - 1], v32[:, :, :, :]).then_inc(v_ready, 1)
                    dve.wait_ge(v_ready, b + 1)
                c.end()
            loop(dve, B // 2, turn)

        @block.gpsimd
        def _(pool):
            pool.wait_ge(xn_ready, B)
            nc.gpsimd.tensor_tensor(m.x_sb[:, :, :], m.x_sb[:, :, :], m.bp_bc[:, :].unsqueeze(1).to_broadcast([P, TILES, D]), ALU.add).then_inc(xb_done, 1)
            pool.wait_ge(xb_done, 1)

        @block.scalar
        def _(act):
            def turn(t):
                for s in range(2):
                    b = t * 2 + s
                    act.wait_ge(x_T, b + 1)
                    if positive(b - 1):
                        act.wait_ge(v_done, b - 1)
                    if positive(b - 1):
                        act.wait_ge(xl_ready, b - 1)
                    nc.scalar.activation(xst[:, s, :], m.psum[s][:, :], ACT.Copy).then_inc(xst_ready, 1)
                    nc.scalar.activation(m.xh[:, seg(b, N)], m.psum[s][:, :], ACT.Copy).then_inc(xh_ready, 1)
            loop(act, B // 2, turn)

        @block.tensor
        def _(pe):
            def turn(t):
                for s in range(2):
                    b = t * 2 + s
                    pe.wait_ge(xn_ready, b + 1)
                    if positive(b - 1):
                        pe.wait_ge(xh_ready, b - 1)
                    for i in range(TB):
                        last = nc.tensor.transpose(m.psum[s][:, i * P:(i + 1) * P], xn[:, s, i, :], m.ident[:, :])
                    last.then_inc(x_T, 1)
                for s in range(2):
                    b = t * 2 + s
                    pe.wait_ge(xst_ready, b + 1)
                    if positive(b - 1):
                        pe.wait_ge(v_ready, b - 1)
                    for i in range(TB):
                        last = nc.tensor.matmul(m.psum[2 + s][:, i * P:(i + 1) * P], xst[:, s, i * P:(i + 1) * P], m.wv[:, :], start=True, stop=True)
                    last.then_inc(v_done, 1)
            loop(pe, B // 2, turn)


PE_STAGES = (("s", 3), ("t", 5), ("o", 8), ("q", 0))
ACT_STAGES = (("t", 6), ("q", 1), ("s", 4))
DVE_STAGES = (("q", 2), ("o", 9), ("t", 7), ("s", 3))


def attention(nc, m, ctx):
    sb, sem = tiles(nc, ctx), nc.alloc_semaphore
    mst = sb("mst", [P, 2, 2 * D], F32R)
    bst = sb("bst", [P, 2], F32)
    vst = sb("vst", [P, 2, TB, VC], BF16)
    qh = [sb(f"qh{k}", [P, N], F32R) for k in range(2)]
    ql = [sb(f"ql{k}", [P, N], F32R) for k in range(2)]
    nmax = sb("nmax", [P, 3, 2], F32)
    p_sb = [sb(f"p_sb{k}", [P, N], F32) for k in range(3)]
    pTh = [sb(f"pTh{k}", [P, N], F16) for k in range(6)]
    pTl = [sb(f"pTl{k}", [P, N], F16) for k in range(6)]
    S_BANK, T_BANK, Q_BANK, O_BANK = (0, 1, 2), (3, 4, 5), 6, 7
    STEP_TILES = (((0, 0), (1, P)), ((2, 0),), ((3, 0),))
    SH = len(STEP_TILES)
    ST = 2 * SH

    def width(j):
        return sum((i + 1) * P for i, _ in STEP_TILES[j])

    m_staged = sem("m_staged")
    v_staged = sem("v_staged")
    q_done = sem("q_done")
    qh_ready = sem("qh_ready")
    ql_ready = sem("ql_ready")
    s_done = sem("s_done")
    max_ready = sem("max_ready")
    exp_done = sem("exp_done")
    t_done = sem("t_done")
    pTh_ready = sem("pTh_ready")
    pTl_ready = sem("pTl_ready")
    pv_done = sem("pv_done")
    o_ready = sem("o_ready")

    TURNS = B * H // 2

    def turn_slots(turn, stages, emit):
        for s in range(ST):
            for stage, lag in stages:
                back, r = divmod(s - lag, ST)
                own = turn + back
                if isinstance(own, int) and not 0 <= own < TURNS:
                    continue
                emit(stage, own * ST + r, own * 2 + r // SH, own, r)

    def run(eng, stages, emit):
        turn_slots(0, stages, emit)
        turn_slots(1, stages, emit)
        turn_slots(2, stages, emit)
        with nc.Fori(3, TURNS, engines=(eng.engine,), hint_back_edge=True) as turn:
            turn_slots(turn, stages, emit)
        turn_slots(TURNS, stages, emit)
        turn_slots(TURNS + 1, stages, emit)

    with nc.Block() as block:

        @block.gpsimd
        def _(pool):
            def stage_m(turn, k):
                h, g = (turn % (H // 2)) * 2 + k, turn * 2 + k
                if positive(g - 1):
                    pool.wait_ge(ql_ready, g - 1)
                nc.gpsimd.tensor_copy(mst[:, k, 0:D], f(m.mh[:, one_of(h), :]))
                nc.gpsimd.tensor_copy(mst[:, k, D:2 * D], f(m.ml[:, one_of(h), :]))
                nc.gpsimd.tensor_copy(bst[:, k:k + 1], m.bq[:, one_of(h)]).then_inc(m_staged, 1)

            def stage_v(turn, k):
                b, h, g = turn // (H // 2), (turn % (H // 2)) * 2 + k, turn * 2 + k
                if positive((g - 1) * SH):
                    pool.wait_ge(pv_done, (g - 1) * SH)
                nc.gpsimd.tensor_copy(vst[:, k, :, :], m.v_sb[:, seg(b, TB), seg(h, VC)]).then_inc(v_staged, 1)

            for k in range(2):
                stage_m(0, k)
            for k in range(2):
                stage_m(1, k)
                stage_v(0, k)
            with nc.Fori(2, TURNS, engines=(pool.engine,), hint_back_edge=True) as turn:
                for k in range(2):
                    stage_m(turn, k)
                    stage_v(turn - 1, k)
            for k in range(2):
                stage_v(TURNS - 1, k)

        @block.tensor
        def _(pe):
            def emit(stage, u, g, turn, r):
                k, j = r // SH, r % SH
                b = turn // (H // 2)
                if stage == "q" and j == 0:
                    pe.wait_ge(m_staged, g + 1)
                    if positive(g):
                        pe.wait_ge(ql_ready, g)
                    x_h, x_l = m.xh[:, seg(b, N)], m.xl[:, seg(b, N)]
                    bank = m.psum[Q_BANK][:, :]
                    nc.tensor.matmul(bank, mst[:, k, 0:D], x_h, start=True, stop=False)
                    nc.tensor.matmul(bank, mst[:, k, 0:D], x_l, start=False, stop=False)
                    nc.tensor.matmul(bank, mst[:, k, D:2 * D], x_h, start=False, stop=True).then_inc(q_done, 1)
                if stage == "s":
                    if j == 0:
                        pe.wait_ge(ql_ready, g + 1)
                    if positive(u - 2):
                        pe.wait_ge(exp_done, u - 2)
                    for i, at in STEP_TILES[j]:
                        w = (i + 1) * P
                        x_h, x_l = m.xh[:, seg(b, N, w)], m.xl[:, seg(b, N, w)]
                        q_h, q_l = (q[k][:, i * P:(i + 1) * P] for q in (qh, ql))
                        bank = m.psum[S_BANK[r % 3]][:, at:at + w]
                        nc.tensor.matmul(bank, q_h, x_h, start=True, stop=False)
                        nc.tensor.matmul(bank, q_h, x_l, start=False, stop=False)
                        nc.tensor.matmul(bank[:, i * P:w], m.ident_b[:, :], m.mask_b[:, :], start=False, stop=False)
                        last = nc.tensor.matmul(bank, q_l, x_h, start=False, stop=True)
                    last.then_inc(s_done, 1)
                if stage == "t":
                    pe.wait_ge(exp_done, u + 1)
                    if positive(u - 2):
                        pe.wait_ge(pTl_ready, u - 2)
                    for c in range(0, width(j), P):
                        last = nc.tensor.transpose(m.psum[T_BANK[r % 3]][:, c:c + P], p_sb[r % 3][:, c:c + P], m.ident[:, :])
                    last.then_inc(t_done, 1)
                if stage == "o":
                    if j == 0:
                        pe.wait_ge(v_staged, g + 1)
                        if positive(g):
                            pe.wait_ge(o_ready, g)
                    pe.wait_ge(pTl_ready, u + 1)
                    for i, at in STEP_TILES[j]:
                        for c in range(i + 1):
                            for part in (pTh, pTl):
                                last = nc.tensor.matmul(m.psum[O_BANK][:, i * VC:(i + 1) * VC], part[r][:, at + c * P:at + (c + 1) * P], vst[:, k, c, :],
                                                        start=(c == 0 and part is pTh), stop=(c == i and part is pTl))
                    last.then_inc(pv_done, 1)
            run(pe, PE_STAGES, emit)

        @block.scalar
        def _(act):
            def emit(stage, u, g, turn, r):
                k, j = r // SH, r % SH
                if stage == "q" and j == 0:
                    act.wait_ge(q_done, g + 1)
                    if positive((g - 1) * SH):
                        act.wait_ge(s_done, (g - 1) * SH)
                    nc.scalar.activation(qh[k][:, :], m.psum[Q_BANK][:, :], ACT.Identity, bias=bst[:, k:k + 1]).then_inc(qh_ready, 1)
                if stage == "s":
                    act.wait_ge(max_ready, u + 1)
                    if positive(u - 2):
                        act.wait_ge(t_done, u - 2)
                    for n, (i, at) in enumerate(STEP_TILES[j]):
                        w = (i + 1) * P
                        last = nc.scalar.activation(p_sb[r % 3][:, at:at + w], m.psum[S_BANK[r % 3]][:, at:at + w], ACT.Exp, bias=nmax[:, r % 3, n:n + 1])
                    last.then_inc(exp_done, 1)
                if stage == "t":
                    w = width(j)
                    act.wait_ge(t_done, u + 1)
                    if positive(u - 5):
                        act.wait_ge(pv_done, u - 5)
                    nc.scalar.activation(pTh[r][:, 0:w], m.psum[T_BANK[r % 3]][:, 0:w], ACT.Copy, scale=LIFT).then_inc(pTh_ready, 1)
            run(act, ACT_STAGES, emit)

        @block.vector
        def _(dve):
            def emit(stage, u, g, turn, r):
                k, j = r // SH, r % SH
                if stage == "q" and j == 0:
                    dve.wait_ge(qh_ready, g + 1)
                    if positive((g - 1) * SH):
                        dve.wait_ge(s_done, (g - 1) * SH)
                    nc.vector.scalar_tensor_tensor(out=ql[k][:, :], in0=m.psum[Q_BANK][:, :], scalar=bst[:, k:k + 1], in1=f(qh[k][:, :]), op0=ALU.add, op1=ALU.subtract).then_inc(ql_ready, 1)
                if stage == "s":
                    dve.wait_ge(s_done, u + 1)
                    if positive(u - 2):
                        dve.wait_ge(exp_done, u - 2)
                    for n, (i, at) in enumerate(STEP_TILES[j]):
                        last = nc.vector.tensor_reduce(out=nmax[:, r % 3, n:n + 1], in_=m.psum[S_BANK[r % 3]][:, at:at + (i + 1) * P], axis=AX.X, op=ALU.max, negate=True)
                    last.then_inc(max_ready, 1)
                if stage == "t":
                    w = width(j)
                    dve.wait_ge(pTh_ready, u + 1)
                    if positive(u - 5):
                        dve.wait_ge(pv_done, u - 5)
                    nc.vector.scalar_tensor_tensor(out=pTl[r][:, 0:w], in0=m.psum[T_BANK[r % 3]][:, 0:w], scalar=LIFT, in1=pTh[r][:, 0:w], op0=ALU.mult, op1=ALU.subtract).then_inc(pTl_ready, 1)
                if stage == "o" and j == SH - 1:
                    b = turn // (H // 2)
                    h = (turn % (H // 2)) * 2 + k
                    dve.wait_ge(pv_done, u + 1)
                    nc.vector.tensor_reduce(out=m.o_sb[:, seg(b, TB), seg(h, V1)], in_=m.psum[O_BANK][:, 0:TB * VC].rearrange("p (t c k) -> p t c k", t=TB, k=PARTS), axis=AX.X, op=ALU.add).then_inc(o_ready, 1)
            run(dve, DVE_STAGES, emit)


def after_attention(nc, m, ctx):
    sb, sem = tiles(nc, ctx), nc.alloc_semaphore
    rinv = sb("rinv", [P, 2, TB, H], F32)
    on = sb("on", [P, 2, TB, D], F32)
    onT = sb("onT", [P, 2, N], F32)
    hn = sb("hn", [P, 2, TB, D], F32)
    hst = sb("hst", [P, 2, N], F32)
    bn = sb("bn2", [P, 2 * TB, 6], F32)
    mv = sb("mv2", [P, 2 * TB, 2], F32)
    var = sb("var2", [P, 2 * TB], F32)
    rstd = sb("rstd2", [P, 2 * TB], F32)
    tmp = sb("tmp2", [P, 2 * TB], F32)
    lg = sb("lg", [P, 2, TB, E], F32)
    ex = sb("ex", [P, 2 * TB, E], F32)
    pr = sb("pr", [P, 2 * TB, E], F32)
    p2 = sb("p2", [P, 2 * TB, E], F32)
    eq = sb("eq", [P, 2 * TB, E], F32)
    sel = sb("sel", [P, 2, 2 * TB, E], F32)
    top = sb("top", [P, 4, 2 * TB], F32)
    w_sb = sb("w_sb", [P, 2 * TB, E], F32)
    wT_sb = sb("wT_sb", [E, 2, N], F32)
    names = ("on_ready", "on_T", "onT_ready", "proj_done", "hn_ready", "h_T", "hst_ready", "hh_ready", "hl_ready",
             "logits_done", "lg_ready", "ex_ready", "w_ready", "w_T2", "wT_ready", "w_stored", "dve_chain3")
    (on_ready, on_T, onT_ready, proj_done, hn_ready, h_T, hst_ready, hh_ready, hl_ready,
     logits_done, lg_ready, ex_ready, w_ready, w_T2, wT_ready, w_stored, dve_chain) = (sem(n) for n in names)

    def bank(kind, s):
        return m.psum[kind * 2 + s]

    with nc.Block() as block:

        @block.vector
        def _(dve):
            def turn(t):
                c = Chain(dve, dve_chain, t, CHAIN3)
                for s in range(2):
                    o = m.o_sb[:, seg(t * 2 + s, TB), :].rearrange("p t (h d) -> p t h d", h=H)
                    c.link(nc.vector.reciprocal(rinv[:, s, :, :], o[:, :, :, DH]))
                for s in range(2):
                    o = m.o_sb[:, seg(t * 2 + s, TB), :].rearrange("p t (h d) -> p t h d", h=H)
                    nc.vector.tensor_tensor(on[:, s, :, :].rearrange("p t (h d) -> p t h d", h=H), o[:, :, :, 0:DH],
                                            rinv[:, s, :, :].unsqueeze(3).to_broadcast([P, TB, H, DH]), ALU.mult).then_inc(on_ready, 1)
                for s in range(2):
                    dve.wait_ge(proj_done, t * 2 + s + 1)
                    xs = m.x_sb[:, seg(t * 2 + s, TB), :]
                    c.link(nc.vector.tensor_tensor(xs, bank(1, s)[:, :].rearrange("p (t d) -> p t d", t=TB), xs, ALU.add))
                if not isinstance(t, int):
                    carry(dve, m)
                for i in range(2 * TB):
                    last = nc.vector.bn_stats(bn[:, i, :], m.x_sb[:, bass.ds(t * 2 * TB + i, 1), :])
                c.link(last)
                if not isinstance(t, int):
                    carry(dve, m)
                for i in range(2 * TB):
                    last = nc.vector.bn_aggr(mv[:, i, :], bn[:, i, :])
                c.link(last)
                c.link(nc.vector.tensor_copy(var[:, :], mv[:, :, 1]))
                rsqrt_steps(nc, c.link, var[:, :], rstd[:, :], tmp[:, :])
                for s in range(2):
                    for i in range(TB):
                        a = s * TB + i
                        last = nc.vector.tensor_scalar(hn[:, s, i, :], m.x_sb[:, bass.ds(t * 2 * TB + a, 1), :], mv[:, a, 0:1], rstd[:, a:a + 1], ALU.subtract, ALU.mult)
                    last.then_inc(hn_ready, 1)
                for s in range(2):
                    dve.wait_ge(hst_ready, t * 2 + s + 1)
                    dve.wait_ge(hh_ready, t * 2 + s + 1)
                    nc.vector.tensor_tensor(m.xl[:, seg(t * 2 + s, N)], hst[:, s, :], f(m.xh[:, seg(t * 2 + s, N)]), ALU.subtract).then_inc(hl_ready, 1)
                for s in range(2):
                    dve.wait_ge(logits_done, t * 2 + s + 1)
                    nc.vector.tensor_tensor(lg[:, s, :, :], bank(2, s)[:, 0:TB * E].rearrange("p (t e) -> p t e", e=E),
                                            m.rb_bc[:, :].unsqueeze(1).to_broadcast([P, TB, E]), ALU.add).then_inc(lg_ready, 1)
                dve.wait_ge(ex_ready, t + 1)
                c.link(nc.vector.tensor_scalar(ex[:, :, :], ex[:, :, :], 1.0, None, ALU.add))
                c.link(nc.vector.reciprocal(pr[:, :, :], ex[:, :, :]))
                src = pr
                for k in range(2):
                    best, first = top[:, 2 * k, :], top[:, 2 * k + 1, :]
                    c.link(nc.vector.tensor_reduce(out=best, in_=src[:, :, :], axis=AX.X, op=ALU.max))
                    c.link(nc.vector.tensor_tensor(eq[:, :, :], src[:, :, :], best.unsqueeze(2).to_broadcast([P, 2 * TB, E]), ALU.is_equal))
                    c.link(nc.vector.tensor_tensor(eq[:, :, :], eq[:, :, :], m.order[:, :, :], ALU.mult))
                    c.link(nc.vector.tensor_reduce(out=first, in_=eq[:, :, :], axis=AX.X, op=ALU.max))
                    c.link(nc.vector.tensor_tensor(sel[:, k, :, :], m.order[:, :, :], first.unsqueeze(2).to_broadcast([P, 2 * TB, E]), ALU.is_equal))
                    if k == 0:
                        c.link(nc.vector.scalar_tensor_tensor(out=p2[:, :, :], in0=sel[:, 0, :, :], scalar=-2.0, in1=pr[:, :, :], op0=ALU.mult, op1=ALU.add))
                        src = p2
                c.link(nc.vector.tensor_tensor(eq[:, :, :], sel[:, 0, :, :], sel[:, 1, :, :], ALU.add))
                c.link(nc.vector.tensor_tensor(eq[:, :, :], eq[:, :, :], pr[:, :, :], ALU.mult))
                c.link(nc.vector.tensor_tensor(top[:, 1, :], top[:, 0, :], top[:, 2, :], ALU.add))
                c.link(nc.vector.reciprocal(top[:, 3, :], top[:, 1, :]))
                nc.vector.tensor_tensor(w_sb[:, :, :], eq[:, :, :], top[:, 3, :].unsqueeze(2).to_broadcast([P, 2 * TB, E]), ALU.mult).then_inc(w_ready, 1)
                c.end()
            loop(dve, B // 2, turn)

        @block.tensor
        def _(pe):
            def turn(t):
                for s in range(2):
                    pe.wait_ge(on_ready, t * 2 + s + 1)
                    for i in range(TB):
                        last = nc.tensor.transpose(bank(0, s)[:, i * P:(i + 1) * P], on[:, s, i, :], m.ident[:, :])
                    last.then_inc(on_T, 1)
                for s in range(2):
                    pe.wait_ge(onT_ready, t * 2 + s + 1)
                    for i in range(TB):
                        last = nc.tensor.matmul(bank(1, s)[:, i * P:(i + 1) * P], onT[:, s, i * P:(i + 1) * P], m.wp[:, :], start=True, stop=True)
                    last.then_inc(proj_done, 1)
                for s in range(2):
                    pe.wait_ge(hn_ready, t * 2 + s + 1)
                    for i in range(TB):
                        last = nc.tensor.transpose(bank(0, s)[:, i * P:(i + 1) * P], hn[:, s, i, :], m.ident[:, :])
                    last.then_inc(h_T, 1)
                for s in range(2):
                    pe.wait_ge(hst_ready, t * 2 + s + 1)
                    for i in range(TB):
                        last = nc.tensor.matmul(bank(2, s)[:, i * E:(i + 1) * E], hst[:, s, i * P:(i + 1) * P], m.rwT[:, :], start=True, stop=True)
                    last.then_inc(logits_done, 1)
                pe.wait_ge(w_ready, t + 1)
                for s in range(2):
                    if positive(t * 2):
                        pe.wait_ge(wT_ready, t * 2)
                    for i in range(TB):
                        last = nc.tensor.transpose(bank(3, s)[0:E, i * P:(i + 1) * P], w_sb[:, s * TB + i, :], m.ident[:, :])
                    last.then_inc(w_T2, 1)
            loop(pe, B // 2, turn)

        @block.scalar
        def _(act):
            def turn(t):
                for s in range(2):
                    act.wait_ge(on_T, t * 2 + s + 1)
                    nc.scalar.activation(onT[:, s, :], bank(0, s)[:, :], ACT.Copy).then_inc(onT_ready, 1)
                for s in range(2):
                    act.wait_ge(h_T, t * 2 + s + 1)
                    if positive(t * 2):
                        act.wait_ge(hl_ready, t * 2)
                    nc.scalar.activation(hst[:, s, :], bank(0, s)[:, :], ACT.Copy).then_inc(hst_ready, 1)
                    nc.scalar.activation(m.xh[:, seg(t * 2 + s, N)], bank(0, s)[:, :], ACT.Copy).then_inc(hh_ready, 1)
                act.wait_ge(lg_ready, t * 2 + 2)
                nc.scalar.activation(ex[:, :, :], lg[:, :, :, :].rearrange("p s t e -> p (s t) e"), ACT.Exp, scale=-1.0).then_inc(ex_ready, 1)
                for s in range(2):
                    act.wait_ge(w_T2, t * 2 + s + 1)
                    if positive(t * 32):
                        act.wait_ge(w_stored, t * 32)
                    nc.scalar.activation(wT_sb[:, s, :], bank(3, s)[0:E, :], ACT.Copy).then_inc(wT_ready, 1)
            loop(act, B // 2, turn)

        @block.sync
        def _(sp):
            def turn(t):
                for s in range(2):
                    sp.wait_ge(wT_ready, t * 2 + s + 1)
                    sp.dma_start(m.w_dram[:, seg(t * 2 + s, N)], wT_sb[:, s, :]).then_inc(w_stored, 16)
            loop(sp, B // 2, turn)
            sp.wait_ge(w_stored, 16 * B)


CHAIN3 = 2 + 2 + 1 + 1 + 1 + RSQRT_LINKS + 2 + 11 + 4


def experts(nc, m, ctx):
    sb, sem = tiles(nc, ctx), nc.alloc_semaphore
    wbc = [sb(f"wbc{s}", [P, TOK], F32) for s in range(2)]
    y = m.v_sb[:, :, :].rearrange("p t c -> p (t c)")[:, 0:2 * TOK].bitcast(F32)
    sg = sb("sg", [P, 2, N], F32)
    su = sb("su", [P, 2, N], F32)
    gu = [sb(f"gu{s}", [P, 2, N], F32) for s in range(2)]
    guh = [[sb(f"guh{s}{k}", [P, N], F32R) for k in range(2)] for s in range(2)]
    gul = [[sb(f"gul{s}{k}", [P, N], F32R) for k in range(2)] for s in range(2)]
    yst = sb("yst", [P, 2, N], F32)
    out_sb = sb("out_sb", [P, 2, TB, D], F32)
    w_loaded = [sem(f"w_loaded{s}") for s in range(2)]
    wbc_loaded = [sem(f"wbc_loaded{s}") for s in range(2)]
    wh_ready = sem("wh_ready")
    w_split = sem("w_split")
    ones_made = sem("ones_made")
    y_zero = sem("y_zero")
    gate_up = sem("gate_up")
    silu_ready = sem("silu_ready")
    su_ready = sem("su_ready")
    gu_ready = sem("gu_ready")
    guh_ready = sem("guh_ready")
    gul_ready = sem("gul_ready")
    down_done = sem("down_done")
    y_added = sem("y_added")
    yst_ready, y_T, out_ready, out_stored = (sem(n) for n in ("yst_ready", "y_T", "out_ready", "out_stored"))
    GB, UB, YB = (0, 1), (2, 3), 4
    BATCHES = (E + 1) * B


    def sweep(eng, one, between=None):
        def expert(p, slot):
            for par in range(2):
                one(p, slot, 0 + par, par)
            if between:
                between(p, slot)
            with eng.Fori(1, B // 2) as j:
                for par in range(2):
                    one(p, slot, j * 2 + par, par)
        expert(0, 0)
        with eng.Fori(0, E // 2) as q:
            expert(q * 2 + 1, 1)
            expert(q * 2 + 2, 0)

    with nc.Block() as block:

        @block.sync
        def _(sp):
            def load(e, p, slot):
                if positive(p - 1):
                    sp.wait_ge(w_split, p - 1)
                ei = slice(e, e + 1) if isinstance(e, int) else bass.ds(e, 1)
                sp.dma_start(m.wraw[:, slot, 0:I], m.gate_w[ei, :, :].rearrange("e h i -> h (e i)")).then_inc(w_loaded[slot], 16)
                sp.dma_start(m.wraw[:, slot, I:2 * I], m.up_w[ei, :, :].rearrange("e h i -> h (e i)")).then_inc(w_loaded[slot], 16)
                sp.dma_start(m.wraw[:, slot, 2 * I:EW].rearrange("p (k d) -> p k d", k=2), m.down_w[ei, :, :].rearrange("e (k p) d -> p (e k) d", p=P)).then_inc(w_loaded[slot], 16)
                if positive((p - 1) * 2 * B):
                    sp.wait_ge(gu_ready, (p - 1) * 2 * B)
                sp.dma_start(wbc[slot][:, :], m.w_dram[ei, :].rearrange("e t -> (e t)").partition_broadcast(P)).then_inc(wbc_loaded[slot], 16)
            load(0, 1, 1)
            load(1, 2, 0)
            with sp.Fori(1, E // 2) as q:
                load(q * 2, q * 2 + 1, 1)
                load(q * 2 + 1, q * 2 + 2, 0)
            def turn(t):
                for s in range(2):
                    sp.wait_ge(out_ready, t * 2 + s + 1)
                    sp.dma_start(m.out[bass.ds(t * 2 + s, 1), :, :].rearrange("b (t p) d -> p (b t) d", p=P), out_sb[:, s, :, :]).then_inc(out_stored, 16)
            loop(sp, B // 2, turn)
            sp.wait_ge(out_stored, 16 * B)

        @block.gpsimd
        def _(pool):
            def split(p, slot):
                if positive(p):
                    if positive((p - 1) * B):
                        pool.wait_ge(down_done, (p - 1) * B)
                    pool.wait_ge(w_loaded[slot], ((p - 1) // 2) * 48 + 48)
                nc.gpsimd.tensor_tensor(m.wh[slot][:, :], m.wraw[:, slot, :], m.carrier[:, 0:1].to_broadcast([P, EW]), ALU.add).then_inc(wh_ready, 1)
                pool.wait_ge(wh_ready, p + 1)
                nc.gpsimd.tensor_tensor(m.wl[slot][:, :], m.wraw[:, slot, :], f(m.wh[slot][:, :]), ALU.subtract).then_inc(w_split, 1)

            def one(p, slot, b, par):
                nb = p * B + b
                for k in range(2):
                    pool.wait_ge(guh_ready, nb * 2 + k + 1)
                    if positive(nb - 1):
                        pool.wait_ge(down_done, nb - 1)
                    nc.gpsimd.tensor_tensor(gul[par][k][:, :], gu[par][:, k, :], f(guh[par][k][:, :]), ALU.subtract).then_inc(gul_ready, 1)

            nc.gpsimd.memset(wbc[0][:, :], 1.0).then_inc(ones_made, 1)
            pool.wait_ge(ones_made, 1)
            nc.gpsimd.memset(y, 0.0).then_inc(y_zero, 1)
            split(0, 0)
            def expert(p, slot, last=False):
                for par in range(2):
                    one(p, slot, par, par)
                if not last:
                    split(p + 1, 1 - slot)
                with pool.Fori(1, B // 2) as j:
                    for par in range(2):
                        one(p, slot, j * 2 + par, par)
            expert(0, 0)
            with pool.Fori(0, E // 2 - 1) as q:
                expert(q * 2 + 1, 1)
                expert(q * 2 + 2, 0)
            expert(E - 1, 1)
            expert(E, 0, last=True)

        @block.tensor
        def _(pe):
            def down(slot, n_batch, par):
                if positive(n_batch):
                    pe.wait_ge(y_added, n_batch)
                for k in range(2):
                    pe.wait_ge(gul_ready, n_batch * 2 + k + 1)
                    w_h = m.wh[slot][:, 2 * I + k * D:2 * I + (k + 1) * D]
                    w_l = m.wl[slot][:, 2 * I + k * D:2 * I + (k + 1) * D]
                    nc.tensor.matmul(m.psum[YB][:, :], w_h, guh[par][k][:, :], start=(k == 0), stop=False)
                    nc.tensor.matmul(m.psum[YB][:, :], w_h, gul[par][k][:, :], start=False, stop=False)
                    last = nc.tensor.matmul(m.psum[YB][:, :], w_l, guh[par][k][:, :], start=False, stop=(k == 1))
                last.then_inc(down_done, 1)

            def one(p, slot, b, par):
                nb = p * B + b
                if isinstance(b, int) and b == 0:
                    pe.wait_ge(w_split, p + 1)
                x_h, x_l = m.xh[:, seg(b, N)], m.xl[:, seg(b, N)]
                for k in range(2):
                    if positive(nb * 2 + k - 1):
                        pe.wait_ge(su_ready, nb * 2 + k - 1)
                    for c, banks in ((0, GB), (1, UB)):
                        w_h = m.wh[slot][:, c * I + k * P:c * I + (k + 1) * P]
                        w_l = m.wl[slot][:, c * I + k * P:c * I + (k + 1) * P]
                        bank = m.psum[banks[k]][:, :]
                        nc.tensor.matmul(bank, w_h, x_h, start=True, stop=False)
                        nc.tensor.matmul(bank, w_h, x_l, start=False, stop=False)
                        last = nc.tensor.matmul(bank, w_l, x_h, start=False, stop=True)
                    last.then_inc(gate_up, 1)
                if isinstance(b, int) and b == 0:
                    if positive(p):
                        down(1 - slot, nb - 1, 1)
                else:
                    down(slot, nb - 1, 1 - par)
            sweep(pe, one)
            down(0, BATCHES - 1, 1)
            def turn(t):
                for s in range(2):
                    pe.wait_ge(yst_ready, t * 2 + s + 1)
                    if positive(t * 2):
                        pe.wait_ge(out_ready, t * 2)
                    for i in range(TB):
                        last = nc.tensor.transpose(m.psum[5 + s][:, i * P:(i + 1) * P], yst[:, s, i * P:(i + 1) * P], m.ident[:, :])
                    last.then_inc(y_T, 1)
            loop(pe, B // 2, turn)

        @block.scalar
        def _(act):
            def one(p, slot, b, par):
                nb = p * B + b
                for k in range(2):
                    n = nb * 2 + k
                    act.wait_ge(gate_up, n + 1)
                    if positive(n - 1):
                        act.wait_ge(su_ready, n - 1)
                    nc.scalar.activation(sg[:, k, :], m.psum[GB[k]][:, :], ACT.Silu).then_inc(silu_ready, 1)
                for k in range(2):
                    n = nb * 2 + k
                    act.wait_ge(gu_ready, n + 1)
                    if positive(nb - 1):
                        act.wait_ge(down_done, nb - 1)
                    nc.scalar.activation(guh[par][k][:, :], gu[par][:, k, :], ACT.Copy).then_inc(guh_ready, 1)
            sweep(act, one)
            def turn(t):
                for s in range(2):
                    act.wait_ge(y_added, BATCHES)
                    if positive(t * 2):
                        act.wait_ge(y_T, t * 2)
                    nc.scalar.activation(yst[:, s, :], y[:, seg(t * 2 + s, N)], ACT.Copy).then_inc(yst_ready, 1)
            loop(act, B // 2, turn)

        @block.vector
        def _(dve):
            def add_y(nb, b):
                dve.wait_ge(down_done, nb + 1)
                if isinstance(nb, int) and nb == 0:
                    dve.wait_ge(y_zero, 1)
                ys = y[:, seg(b, N)]
                nc.vector.tensor_tensor(ys, m.psum[YB][:, :], ys, ALU.add).then_inc(y_added, 1)

            def one(p, slot, b, par):
                nb = p * B + b
                if isinstance(b, int) and b == 0:
                    if isinstance(p, int) and p == 0:
                        dve.wait_ge(ones_made, 1)
                    else:
                        dve.wait_ge(wbc_loaded[slot], ((p - 1) // 2) * 16 + 16)
                for k in range(2):
                    n = nb * 2 + k
                    dve.wait_ge(silu_ready, n + 1)
                    if positive(n - 1):
                        dve.wait_ge(gu_ready, n - 1)
                    nc.vector.tensor_tensor(su[:, k, :], m.psum[UB[k]][:, :], sg[:, k, :], ALU.mult).then_inc(su_ready, 1)
                for k in range(2):
                    n = nb * 2 + k
                    dve.wait_ge(su_ready, n + 1)
                    if positive(n - 3):
                        dve.wait_ge(gul_ready, n - 3)
                    nc.vector.tensor_tensor(gu[par][:, k, :], su[:, k, :], wbc[slot][:, seg(b, N)], ALU.mult).then_inc(gu_ready, 1)
                if isinstance(b, int) and b == 0:
                    if positive(p):
                        add_y(nb - 1, B - 1)
                else:
                    add_y(nb - 1, b - 1)
            sweep(dve, one)
            add_y(BATCHES - 1, B - 1)
            def turn(t):
                for s in range(2):
                    dve.wait_ge(y_T, t * 2 + s + 1)
                    if positive(t * 32):
                        dve.wait_ge(out_stored, t * 32)
                    nc.vector.tensor_tensor(out_sb[:, s, :, :], m.psum[5 + s][:, :].rearrange("p (t d) -> p t d", t=TB), m.x_sb[:, seg(t * 2 + s, TB), :], ALU.add).then_inc(out_ready, 1)
            loop(dve, B // 2, turn)


def layer(nc, io):
    m = Mem(nc, io)
    for phase in (prepare, first_norm, attention, after_attention, experts):
        with ExitStack() as ctx:
            phase(nc, m, ctx)


_INS = {"L0_attn_x": "x", "L0_attn_Wkqv": "Wkqv", "L0_attn_bkqv": "bkqv", "L0_attn_Wp": "Wp", "L0_attn_bp": "bp",
        "L0_ffn_shared_gate": "shared_gate", "L0_ffn_shared_up": "shared_up", "L0_ffn_shared_down": "shared_down",
        "L0_ffn_gate_w": "gate_w", "L0_ffn_up_w": "up_w", "L0_ffn_down_w": "down_w",
        "L0_ffn_router_w": "router_w", "L0_ffn_routing_bias": "routing_bias"}


def kernel(**inputs):
    import concourse.bacc as bacc
    from concourse.bass_utils import run_bass_kernel_spmd as run

    nc = bacc.Bacc("TRN2", target_bir_lowering=False, num_devices=1)
    arrays, io = {}, []
    for name, short in _INS.items():
        a = np.ascontiguousarray(inputs[name])
        arrays[f"in_{short}"] = a
        io.append(nc.dram_tensor(f"in_{short}", a.shape, mybir.dt.from_np(a.dtype), kind="ExternalInput").ap())
    io.append(nc.dram_tensor("out", (B, N, D), F32, kind="ExternalOutput").ap())
    io.append(nc.dram_tensor("w_dram", (E, TOK), F32, kind="Internal").ap())
    layer(nc, io)
    r = run(nc, [arrays], core_ids=[0])
    return r.results[0]["out"]
```

```python
import concourse.bass as bass
from concourse import mybir
import numpy as np
from contextlib import ExitStack

F32 = mybir.dt.float32
F32R = mybir.dt.float32r
BF16 = mybir.dt.bfloat16
F16 = mybir.dt.float16
I32 = mybir.dt.int32
ALU = mybir.AluOpType
ACT = mybir.ActivationFunctionType
AX = mybir.AxisListType

P = 128
B, N, D = 8, 512, 128
H, DH = 16, 8
E, I = 8, 256
TB = N // P
TOK = B * N
TILES = B * TB
KQV = 2 * D + DH
V1 = DH + 1
PARTS = 3
VC = V1 * PARTS
LIFT = 32768.0
EW = 2 * I + 2 * D
SCALE = float(D) ** -0.5
EPS = 1e-5
MASKED = -1e30
RSQRT_MAGIC = float(0x5F3759DF)


def f(ap):
    return ap.bitcast(F32)


def seg(i, n, width=None):
    width = n if width is None else width
    return slice(i * n, i * n + width) if isinstance(i, int) else bass.ds(i * n, width)


def one_of(i):
    return slice(i, i + 1) if isinstance(i, int) else bass.ds(i, 1)


def tiles(nc, ctx):
    return lambda name, shape, dtype: ctx.enter_context(nc.sbuf_tensor(name, shape, dtype))


def positive(value):
    return not isinstance(value, int) or value > 0


def carry(eng, m):
    m.carriers += 1
    eng.memset(m.carrier[:, m.carriers:m.carriers + 1], 0.0)


def loop(eng, turns, body):
    body(0)
    with eng.Fori(1, turns) as t:
        body(t)


class Chain:

    def __init__(self, eng, sem, turn, per):
        self.eng, self.sem, self.base, self.n, self.per = eng, sem, turn * per, 0, per

    def link(self, ins):
        ins.then_inc(self.sem, 1)
        self.n += 1
        self.eng.wait_ge(self.sem, self.base + self.n)

    def end(self):
        assert self.n == self.per, (self.n, self.per)


RSQRT_STEPS = 3
RSQRT_LINKS = 3 + 4 * RSQRT_STEPS


def rsqrt_steps(nc, link, v, y, t):
    link(nc.vector.tensor_scalar(v, v, EPS, None, ALU.add))
    link(nc.vector.tensor_scalar(t.bitcast(I32), v.bitcast(I32), 1, None, ALU.logical_shift_right))
    link(nc.vector.tensor_scalar(y.bitcast(I32), t.bitcast(I32), -1.0, RSQRT_MAGIC, ALU.mult, ALU.add))
    for _ in range(RSQRT_STEPS):
        link(nc.vector.tensor_tensor(t, y, y, ALU.mult))
        link(nc.vector.tensor_tensor(t, t, v, ALU.mult))
        link(nc.vector.tensor_scalar(t, t, -0.5, 1.5, ALU.mult, ALU.add))
        link(nc.vector.tensor_tensor(y, y, t, ALU.mult))




class Mem:

    def __init__(self, nc, io):
        (self.x, self.Wkqv, self.bkqv, self.Wp, self.bp, self.shared_gate, self.shared_up, self.shared_down, self.gate_w,
         self.up_w, self.down_w, self.router_w, self.routing_bias, self.out, self.w_dram) = io
        sb = nc.alloc_sbuf_tensor
        self.carrier = sb("carrier", [P, 64], F32)
        self.carriers = 0
        self.one = sb("one", [P, 1], F32)
        self.ident = sb("ident", [P, P], F32)
        self.ident_b = sb("ident_b", [P, P], BF16)
        self.mask_b = sb("mask_b", [P, P], BF16)
        self.bv_bc = sb("bv_bc", [P, H, DH], F32)
        self.bp_bc = sb("bp_bc", [P, D], F32)
        self.rb_bc = sb("rb_bc", [P, E], F32)
        self.order = sb("order", [P, TILES, E], F32)
        self.x_sb = sb("x_sb", [P, TILES, D], F32)
        self.xh = sb("xh", [P, TOK], F32R)
        self.xl = sb("xl", [P, TOK], F32R)
        self.v_sb = sb("v_sb", [P, TILES, H * VC], BF16)
        self.y = self.v_sb[:, :, :].rearrange("p t c -> p (t c)")[:, 0:2 * TOK].bitcast(F32)
        self.stats = sb("stats", [P, TILES, 2], F32)
        self.rstd = sb("rstd", [P, TILES], F32)
        self.mh = sb("mh", [P, H, D], F32R)
        self.ml = sb("ml", [P, H, D], F32R)
        self.bq = sb("bq", [P, H], F32)
        self.wv = sb("wv", [P, H * DH], F32)
        self.wp = sb("wp", [P, D], F32)
        self.rwT = sb("rwT", [P, E], F32)
        self.wraw = sb("wraw", [P, 2, EW], F32)
        self.wh = [sb(f"wh{s}", [P, EW], F32R) for s in range(2)]
        self.wl = [sb(f"wl{s}", [P, EW], F32R) for s in range(2)]
        self.psum = [nc.alloc_psum_tensor(f"bank{i}", [P, 512], F32) for i in range(8)]
        self.o_sb = sb("o_sb", [P, TILES, H * V1], F32)


def prepare(nc, m, ctx):
    sb, sem = tiles(nc, ctx), nc.alloc_semaphore
    HG = 2
    LOADS = H // HG
    wst = sb("wst", [P, H, KQV], F32)
    wT = sb("wT", [P, 2, 2 * D], F32)
    bias_rows = sb("bias_rows", [H, KQV], F32)
    bqT = sb("bqT", [P, H], F32)
    rw_rows = sb("rw_rows", [E, D], F32)
    sh_rows = sb("sh_rows", [P, 3, I], F32)
    bn = sb("bn", [P, TILES, 6], F32)
    tmp = sb("tmp_rstd", [P, TILES], F32)
    var = sb("var", [P, TILES], F32)
    xn = sb("xn", [P, TILES, D], F32)
    xst = sb("xst", [P, TOK], F32)
    v32 = sb("v32", [P, TILES, H, DH], F32)
    m32 = f(m.ml[:, :, :])

    x_loaded = [sem(f"x_loaded{b}") for b in range(B)]
    head_loaded = [sem(f"head_loaded{n}") for n in range(LOADS)]
    names = ("bias_loaded", "small_loaded", "shared_loaded", "consts", "masks_made", "wv_copied", "bias_T", "bias_copied",
             "w_T", "w_copied", "m_done", "m_copied", "mh_ready", "ml_ready", "shared_T", "shared_copied", "shared_split",
             "bn_chain0", "dve_chain0", "xn_ready", "x_T", "xst_ready", "xh_ready", "xl_ready", "v_done", "v32_ready",
             "high_ready", "rest_ready", "mid_ready", "low_ready")
    (bias_loaded, small_loaded, shared_loaded, consts, masks_made, wv_copied, bias_T, bias_copied,
     w_T, w_copied, m_done, m_copied, mh_ready, ml_ready, shared_T, shared_copied, shared_split,
     bn_chain, dve_chain, xn_ready, x_T, xst_ready, xh_ready, xl_ready, v_done, v32_ready,
     high_ready, rest_ready, mid_ready, low_ready) = (sem(n) for n in names)

    def value_parts(b):
        return m.v_sb[:, seg(b, TB), :].rearrange("p t (h c k) -> p t h c k", h=H, c=V1)[:, :, :, 0:DH, :]

    with nc.Block() as block:

        @block.sync
        def _(sp):
            sp.dma_start(bias_rows[:, :], m.bkqv).then_inc(bias_loaded, 16)
            sp.dma_start(rw_rows[:, :], m.router_w).then_inc(bias_loaded, 16)
            for n in range(LOADS):
                sp.dma_start(wst[:, seg(n, HG), :], m.Wkqv[n * HG:(n + 1) * HG, :, :].rearrange("h d e -> d h e")).then_inc(head_loaded[n], 16)
            sp.dma_start(m.bv_bc[:, :, :], m.bkqv[:, 2 * D:KQV].partition_broadcast(P)).then_inc(small_loaded, 16)
            sp.dma_start(m.bp_bc[:, :], m.bp.partition_broadcast(P)).then_inc(small_loaded, 16)
            sp.dma_start(m.rb_bc[:, :], m.routing_bias.partition_broadcast(P)).then_inc(small_loaded, 16)
            sp.dma_start(m.wp[:, :], m.Wp).then_inc(small_loaded, 16)
            for k in range(2):
                sp.dma_start(sh_rows[:, k, :].rearrange("p (t d) -> p t d", t=2), (m.shared_gate, m.shared_up)[k].rearrange("(t p) d -> p t d", p=P)).then_inc(shared_loaded, 16)
            sp.dma_start(sh_rows[:, 2, :], m.shared_down).then_inc(shared_loaded, 16)
            sp.wait_ge(small_loaded, 16 * 4)

        @block.scalar
        def _(act):
            for b in range(B):
                act.dma_start(m.x_sb[:, seg(b, TB), :], m.x[b, :, :].rearrange("(t p) d -> p t d", p=P)).then_inc(x_loaded[b], 16)
            act.wait_ge(bias_T, 1)
            nc.scalar.activation(bqT[:, :], m.psum[6][:, 0:H], ACT.Copy)
            nc.scalar.activation(m.rwT[:, :], m.psum[6][:, H:H + E], ACT.Copy).then_inc(bias_copied, 1)
            for h in range(H + 1):
                if h < H:
                    act.wait_ge(w_T, h + 1)
                    if h >= 2:
                        act.wait_ge(m_done, h - 1)
                    nc.scalar.activation(wT[:, h % 2, :], m.psum[h % 2][:, 0:2 * D], ACT.Copy).then_inc(w_copied, 1)
                if h >= 1:
                    act.wait_ge(m_done, h)
                    ps = m.psum[2 + (h - 1) % 2]
                    nc.scalar.activation(m.bq[:, h - 1:h], ps[:, D:D + 1], ACT.Copy, scale=SCALE)
                    nc.scalar.activation(m32[:, h - 1, :], ps[:, 0:D], ACT.Copy, scale=SCALE).then_inc(m_copied, 1)
            for k in range(2):
                act.wait_ge(shared_T, k + 1)
                nc.scalar.activation(m.wraw[:, 0, k * 512:min(EW, k * 512 + 512)], m.psum[4 + k][:, 0:min(512, EW - k * 512)], ACT.Copy).then_inc(shared_copied, 1)
            act.wait_ge(m_copied, H)
            nc.scalar.activation(m.mh[:, :, :], m32, ACT.Copy).then_inc(mh_ready, 1)
            for b in range(B + 2):
                if b < B:
                    act.wait_ge(x_T, b + 1)
                    nc.scalar.activation(xst[:, seg(b, N)], m.psum[b % 4][:, :], ACT.Copy).then_inc(xst_ready, 1)
                    nc.scalar.activation(m.xh[:, seg(b, N)], m.psum[b % 4][:, :], ACT.Copy).then_inc(xh_ready, 1)
                if 0 <= b - 1 < B:
                    act.wait_ge(v32_ready, b)
                    nc.scalar.activation(value_parts(b - 1)[:, :, :, :, 0], v32[:, seg(b - 1, TB), :, :], ACT.Copy).then_inc(high_ready, 1)
                if 0 <= b - 2 < B:
                    act.wait_ge(rest_ready, b - 1)
                    nc.scalar.activation(value_parts(b - 2)[:, :, :, :, 1], v32[:, seg(b - 2, TB), :, :], ACT.Copy).then_inc(mid_ready, 1)

        @block.gpsimd
        def _(pool):
            nc.gpsimd.memset(m.ident[:, :], 0.0).then_inc(consts, 1)
            pool.wait_ge(consts, 1)
            nc.gpsimd.affine_select(out=m.ident[:, :], in_=m.ident[:, :], compare_op=ALU.not_equal, fill=1.0, base=0, pattern=[[-1, P]], channel_multiplier=1).then_inc(masks_made, 1)
            nc.gpsimd.memset(m.ident_b[:, :], 0.0).then_inc(consts, 1)
            nc.gpsimd.memset(m.mask_b[:, :], 0.0).then_inc(consts, 1)
            pool.wait_ge(consts, 3)
            nc.gpsimd.affine_select(out=m.ident_b[:, :], in_=m.ident_b[:, :], compare_op=ALU.not_equal, fill=1.0, base=0, pattern=[[-1, P]], channel_multiplier=1)
            nc.gpsimd.affine_select(out=m.mask_b[:, :], in_=m.mask_b[:, :], compare_op=ALU.is_ge, fill=MASKED, base=0, pattern=[[-1, P]], channel_multiplier=1)
            nc.gpsimd.memset(m.carrier[:, 0:1], 0.0).then_inc(consts, 1)
            nc.gpsimd.memset(m.one[:, :], 1.0)
            ones = m.v_sb[:, :, :].rearrange("p t (h c k) -> p (t h) c k", c=V1, k=PARTS)[:, :, DH, :]
            nc.gpsimd.memset(ones[:, :, 0], 1.0)
            nc.gpsimd.memset(ones[:, :, 1:PARTS], 0.0)
            for e in range(E):
                nc.gpsimd.memset(m.order[:, :, e], float(E - e))
            for n in range(LOADS):
                pool.wait_ge(head_loaded[n], 16)
                nc.gpsimd.tensor_copy(m.wv[:, seg(n, HG * DH)].rearrange("p (h d) -> p h d", h=HG), wst[:, seg(n, HG), 2 * D:KQV]).then_inc(wv_copied, 1)
            pool.wait_ge(shared_copied, 2)
            pool.wait_ge(consts, 4)
            nc.gpsimd.tensor_tensor(m.wh[0][:, :], m.wraw[:, 0, :], m.carrier[:, 0:1].to_broadcast([P, EW]), ALU.add).then_inc(shared_split, 1)
            pool.wait_ge(shared_split, 1)
            nc.gpsimd.tensor_tensor(m.wl[0][:, :], m.wraw[:, 0, :], f(m.wh[0][:, :]), ALU.subtract).then_inc(shared_split, 1)
            for b in range(B):
                pool.wait_ge(high_ready, b + 1)
                v = v32[:, seg(b, TB), :, :]
                nc.gpsimd.tensor_tensor(v, v, value_parts(b)[:, :, :, :, 0], ALU.subtract).then_inc(rest_ready, 1)

        @block.vector
        def _(dve):
            for b in range(B):
                dve.wait_ge(x_loaded[b], 16)
                for t in range(b * TB, (b + 1) * TB):
                    nc.vector.bn_stats(bn[:, t, :], m.x_sb[:, t, :]).then_inc(bn_chain, 1)
            for t in range(TILES):
                dve.wait_ge(bn_chain, t + 1)
                last = nc.vector.bn_aggr(m.stats[:, t, :], bn[:, t, :])
            c = Chain(dve, dve_chain, 0, 2 + RSQRT_LINKS)
            c.link(last)
            c.link(nc.vector.tensor_copy(var[:, :], m.stats[:, :, 1]))
            rsqrt_steps(nc, c.link, var[:, :], m.rstd[:, :], tmp[:, :])
            c.end()
            for t in range(TILES):
                nc.vector.tensor_scalar(xn[:, t, :], m.x_sb[:, t, :], m.stats[:, t, 0:1], m.rstd[:, t:t + 1], ALU.subtract, ALU.mult).then_inc(xn_ready, 1)
            dve.wait_ge(mh_ready, 1)
            nc.vector.tensor_tensor(m.ml[:, :, :], m32, f(m.mh[:, :, :]), ALU.subtract).then_inc(ml_ready, 1)
            dve.wait_ge(small_loaded, 16 * 4)
            for b in range(B + 3):
                if b < B:
                    dve.wait_ge(xst_ready, b + 1)
                    dve.wait_ge(xh_ready, b + 1)
                    nc.vector.tensor_tensor(m.xl[:, seg(b, N)], xst[:, seg(b, N)], f(m.xh[:, seg(b, N)]), ALU.subtract).then_inc(xl_ready, 1)
                    dve.wait_ge(v_done, b + 1)
                    nc.vector.tensor_tensor(v32[:, seg(b, TB), :, :], m.psum[6 + b % 2][:, :].rearrange("p (t h d) -> p t h d", t=TB, h=H),
                                            m.bv_bc[:, :, :].unsqueeze(1).to_broadcast([P, TB, H, DH]), ALU.add).then_inc(v32_ready, 1)
                if 0 <= b - 3 < B:
                    dve.wait_ge(mid_ready, b - 2)
                    parts = value_parts(b - 3)
                    nc.vector.tensor_tensor(parts[:, :, :, :, 2], v32[:, seg(b - 3, TB), :, :], parts[:, :, :, :, 1], ALU.subtract).then_inc(low_ready, 1)

        @block.tensor
        def _(pe):
            pe.wait_ge(masks_made, 1)
            pe.wait_ge(bias_loaded, 32)
            nc.tensor.transpose(m.psum[6][:, 0:H], bias_rows[:, D:2 * D], m.ident[0:H, 0:H])
            nc.tensor.transpose(m.psum[6][:, H:H + E], rw_rows[:, :], m.ident[0:E, 0:E]).then_inc(bias_T, 1)
            for h in range(H + 1):
                if h < H:
                    if h % HG == 0:
                        pe.wait_ge(head_loaded[h // HG], 16)
                    if h >= 2:
                        pe.wait_ge(w_copied, h - 1)
                    for c in range(2):
                        last = nc.tensor.transpose(m.psum[h % 2][:, c * D:(c + 1) * D], wst[:, h, c * D:(c + 1) * D], m.ident[:, :])
                    last.then_inc(w_T, 1)
                if h >= 1:
                    g = h - 1
                    pe.wait_ge(w_copied, g + 1)
                    if g == 0:
                        pe.wait_ge(bias_copied, 1)
                    if g >= 2:
                        pe.wait_ge(m_copied, g - 1)
                    nc.tensor.matmul(m.psum[2 + g % 2][:, 0:D], wT[:, g % 2, D:2 * D], wT[:, g % 2, 0:D], start=True, stop=True)
                    nc.tensor.matmul(m.psum[2 + g % 2][:, D:D + 1], wT[:, g % 2, 0:D], bqT[:, g:g + 1], start=True, stop=True).then_inc(m_done, 1)
            pe.wait_ge(shared_loaded, 48)
            for k in range(6):
                at = k * P
                nc_out = m.psum[4 + at // 512][:, at % 512:at % 512 + P]
                src = sh_rows[:, k // 2, (k % 2) * P:(k % 2) * P + P]
                last = nc.tensor.transpose(nc_out, src, m.ident[:, :])
                if k in (3, 5):
                    last.then_inc(shared_T, 1)
            pe.wait_ge(m_copied, H)
            pe.wait_ge(wv_copied, LOADS)
            for b in range(B + 1):
                if b < B:
                    pe.wait_ge(xn_ready, (b + 1) * TB)
                    if b >= 4:
                        pe.wait_ge(xh_ready, b - 3)
                    for i in range(TB):
                        last = nc.tensor.transpose(m.psum[b % 4][:, i * P:(i + 1) * P], xn[:, b * TB + i, :], m.ident[:, :])
                    last.then_inc(x_T, 1)
                if b >= 1:
                    g = b - 1
                    pe.wait_ge(xst_ready, g + 1)
                    if g >= 2:
                        pe.wait_ge(v32_ready, g - 1)
                    for i in range(TB):
                        last = nc.tensor.matmul(m.psum[6 + g % 2][:, i * P:(i + 1) * P], xst[:, (g * TB + i) * P:(g * TB + i + 1) * P], m.wv[:, :], start=True, stop=True)
                    last.then_inc(v_done, 1)


PE_STAGES = (("q", 0), ("s", 3), ("o", 9), ("t", 6))
ACT_STAGES = (("q", 0), ("s", 4), ("t", 6))
DVE_STAGES = (("q", 2), ("s", 4), ("t", 7), ("o", 9))


def attention(nc, m, ctx):
    sb, sem = tiles(nc, ctx), nc.alloc_semaphore
    mst = sb("mst", [P, 2, 2 * D], F32R)
    bst = sb("bst", [P, 2], F32)
    vst = sb("vst", [P, 2, TB, VC], BF16)
    qh = [sb(f"qh{k}", [P, N], F32R) for k in range(2)]
    ql = [sb(f"ql{k}", [P, N], F32R) for k in range(2)]
    nmax = sb("nmax", [P, 3, 2], F32)
    p_sb = [sb(f"p_sb{k}", [P, N], F32) for k in range(3)]
    pTh = [sb(f"pTh{k}", [P, N], F16) for k in range(6)]
    pTl = [sb(f"pTl{k}", [P, N], F16) for k in range(6)]
    S_BANK, T_BANK, Q_BANK, O_BANK = (0, 1, 2), (3, 4, 5), 6, 7
    STEP_TILES = (((0, 0), (1, P)), ((2, 0),), ((3, 0),))
    SH = len(STEP_TILES)
    ST = 2 * SH

    def width(j):
        return sum((i + 1) * P for i, _ in STEP_TILES[j])

    m_staged = sem("m_staged")
    v_staged = sem("v_staged")
    q_done = sem("q_done")
    qh_ready = sem("qh_ready")
    ql_ready = sem("ql_ready")
    s_done = sem("s_done")
    max_ready = sem("max_ready")
    exp_done = sem("exp_done")
    t_done = sem("t_done")
    pTh_ready = sem("pTh_ready")
    pTl_ready = sem("pTl_ready")
    pv_done = sem("pv_done")
    o_ready = sem("o_ready")
    bias_added = sem("bias_added")

    TURNS = B * H // 2

    def turn_slots(turn, stages, emit):
        for s in range(ST):
            for stage, lag in stages:
                back, r = divmod(s - lag, ST)
                own = turn + back
                if isinstance(own, int) and not 0 <= own < TURNS:
                    continue
                emit(stage, own * ST + r, own * 2 + r // SH, own, r)

    def run(eng, stages, emit):
        turn_slots(0, stages, emit)
        turn_slots(1, stages, emit)
        turn_slots(2, stages, emit)
        with nc.Fori(3, TURNS, engines=(eng.engine,), hint_back_edge=True) as turn:
            turn_slots(turn, stages, emit)
        turn_slots(TURNS, stages, emit)
        turn_slots(TURNS + 1, stages, emit)

    with nc.Block() as block:

        @block.gpsimd
        def _(pool):
            def stage_m(turn, k):
                h, g = (turn % (H // 2)) * 2 + k, turn * 2 + k
                if positive(g - 1):
                    pool.wait_ge(ql_ready, g - 1)
                nc.gpsimd.tensor_copy(mst[:, k, 0:D], f(m.mh[:, one_of(h), :]))
                nc.gpsimd.tensor_copy(mst[:, k, D:2 * D], f(m.ml[:, one_of(h), :]))
                nc.gpsimd.tensor_copy(bst[:, k:k + 1], m.bq[:, one_of(h)]).then_inc(m_staged, 1)

            def stage_v(turn, k):
                b, h, g = turn // (H // 2), (turn % (H // 2)) * 2 + k, turn * 2 + k
                if positive((g - 1) * SH):
                    pool.wait_ge(pv_done, (g - 1) * SH)
                nc.gpsimd.tensor_copy(vst[:, k, :, :], m.v_sb[:, seg(b, TB), seg(h, VC)]).then_inc(v_staged, 1)

            for k in range(2):
                stage_m(0, k)
            for k in range(2):
                stage_m(1, k)
                stage_v(0, k)
            nc.gpsimd.tensor_tensor(m.x_sb[:, :, :], m.x_sb[:, :, :], m.bp_bc[:, :].unsqueeze(1).to_broadcast([P, TILES, D]), ALU.add).then_inc(bias_added, 1)
            pool.wait_ge(bias_added, 1)
            with nc.Fori(2, TURNS, engines=(pool.engine,), hint_back_edge=True) as turn:
                for k in range(2):
                    stage_m(turn, k)
                    stage_v(turn - 1, k)
            for k in range(2):
                stage_v(TURNS - 1, k)

        @block.tensor
        def _(pe):
            def emit(stage, u, g, turn, r):
                k, j = r // SH, r % SH
                b = turn // (H // 2)
                if stage == "q" and j == 0:
                    pe.wait_ge(m_staged, g + 1)
                    if positive(g):
                        pe.wait_ge(ql_ready, g)
                    x_h, x_l = m.xh[:, seg(b, N)], m.xl[:, seg(b, N)]
                    bank = m.psum[Q_BANK][:, :]
                    nc.tensor.matmul(bank, mst[:, k, 0:D], x_h, start=True, stop=False)
                    nc.tensor.matmul(bank, mst[:, k, 0:D], x_l, start=False, stop=False)
                    nc.tensor.matmul(bank, mst[:, k, D:2 * D], x_h, start=False, stop=True).then_inc(q_done, 1)
                if stage == "s":
                    if j == 0:
                        pe.wait_ge(ql_ready, g + 1)
                    if positive(u - 2):
                        pe.wait_ge(exp_done, u - 2)
                    for i, at in STEP_TILES[j]:
                        w = (i + 1) * P
                        x_h, x_l = m.xh[:, seg(b, N, w)], m.xl[:, seg(b, N, w)]
                        q_h, q_l = (q[k][:, i * P:(i + 1) * P] for q in (qh, ql))
                        bank = m.psum[S_BANK[r % 3]][:, at:at + w]
                        nc.tensor.matmul(bank, q_h, x_h, start=True, stop=False)
                        nc.tensor.matmul(bank, q_h, x_l, start=False, stop=False)
                        nc.tensor.matmul(bank[:, i * P:w], m.ident_b[:, :], m.mask_b[:, :], start=False, stop=False)
                        last = nc.tensor.matmul(bank, q_l, x_h, start=False, stop=True)
                    last.then_inc(s_done, 1)
                if stage == "t":
                    pe.wait_ge(exp_done, u + 1)
                    if positive(u - 2):
                        pe.wait_ge(pTl_ready, u - 2)
                    for c in range(0, width(j), P):
                        last = nc.tensor.transpose(m.psum[T_BANK[r % 3]][:, c:c + P], p_sb[r % 3][:, c:c + P], m.ident[:, :])
                    last.then_inc(t_done, 1)
                if stage == "o":
                    if j == 0:
                        pe.wait_ge(v_staged, g + 1)
                        if positive(g):
                            pe.wait_ge(o_ready, g)
                    pe.wait_ge(pTl_ready, u + 1)
                    for i, at in STEP_TILES[j]:
                        for c in range(i + 1):
                            for part in (pTh, pTl):
                                last = nc.tensor.matmul(m.psum[O_BANK][:, i * VC:(i + 1) * VC], part[r][:, at + c * P:at + (c + 1) * P], vst[:, k, c, :],
                                                        start=(c == 0 and part is pTh), stop=(c == i and part is pTl))
                    last.then_inc(pv_done, 1)
            run(pe, PE_STAGES, emit)

        @block.scalar
        def _(act):
            def emit(stage, u, g, turn, r):
                k, j = r // SH, r % SH
                if stage == "q" and j == 0:
                    act.wait_ge(q_done, g + 1)
                    if positive((g - 1) * SH):
                        act.wait_ge(s_done, (g - 1) * SH)
                    nc.scalar.activation(qh[k][:, :], m.psum[Q_BANK][:, :], ACT.Identity, bias=bst[:, k:k + 1]).then_inc(qh_ready, 1)
                if stage == "s":
                    act.wait_ge(max_ready, u + 1)
                    if positive(u - 2):
                        act.wait_ge(t_done, u - 2)
                    for n, (i, at) in enumerate(STEP_TILES[j]):
                        w = (i + 1) * P
                        last = nc.scalar.activation(p_sb[r % 3][:, at:at + w], m.psum[S_BANK[r % 3]][:, at:at + w], ACT.Exp, bias=nmax[:, r % 3, n:n + 1])
                    last.then_inc(exp_done, 1)
                if stage == "t":
                    w = width(j)
                    act.wait_ge(t_done, u + 1)
                    if positive(u - 5):
                        act.wait_ge(pv_done, u - 5)
                    nc.scalar.activation(pTh[r][:, 0:w], m.psum[T_BANK[r % 3]][:, 0:w], ACT.Copy, scale=LIFT).then_inc(pTh_ready, 1)
            run(act, ACT_STAGES, emit)

        @block.vector
        def _(dve):
            def emit(stage, u, g, turn, r):
                k, j = r // SH, r % SH
                if stage == "q" and j == 0:
                    dve.wait_ge(qh_ready, g + 1)
                    if positive((g - 1) * SH):
                        dve.wait_ge(s_done, (g - 1) * SH)
                    nc.vector.scalar_tensor_tensor(out=ql[k][:, :], in0=m.psum[Q_BANK][:, :], scalar=bst[:, k:k + 1], in1=f(qh[k][:, :]), op0=ALU.add, op1=ALU.subtract).then_inc(ql_ready, 1)
                if stage == "s":
                    dve.wait_ge(s_done, u + 1)
                    if positive(u - 2):
                        dve.wait_ge(exp_done, u - 2)
                    for n, (i, at) in enumerate(STEP_TILES[j]):
                        last = nc.vector.tensor_reduce(out=nmax[:, r % 3, n:n + 1], in_=m.psum[S_BANK[r % 3]][:, at:at + (i + 1) * P], axis=AX.X, op=ALU.max, negate=True)
                    last.then_inc(max_ready, 1)
                if stage == "t":
                    w = width(j)
                    dve.wait_ge(pTh_ready, u + 1)
                    if positive(u - 5):
                        dve.wait_ge(pv_done, u - 5)
                    nc.vector.scalar_tensor_tensor(out=pTl[r][:, 0:w], in0=m.psum[T_BANK[r % 3]][:, 0:w], scalar=LIFT, in1=pTh[r][:, 0:w], op0=ALU.mult, op1=ALU.subtract).then_inc(pTl_ready, 1)
                if stage == "o" and j == SH - 1:
                    b = turn // (H // 2)
                    h = (turn % (H // 2)) * 2 + k
                    dve.wait_ge(pv_done, u + 1)
                    nc.vector.tensor_reduce(out=m.o_sb[:, seg(b, TB), seg(h, V1)], in_=m.psum[O_BANK][:, 0:TB * VC].rearrange("p (t c k) -> p t c k", t=TB, k=PARTS), axis=AX.X, op=ALU.add).then_inc(o_ready, 1)
            run(dve, DVE_STAGES, emit)


def after_attention(nc, m, ctx):
    sb, sem = tiles(nc, ctx), nc.alloc_semaphore
    rinv = sb("rinv", [P, TILES, H], F32)
    on = sb("on", [P, 2, TB, D], F32)
    onT = sb("onT", [P, 2, N], F32)
    hn = sb("hn", [P, 2, TB, D], F32)
    hst = sb("hst", [P, 2, N], F32)
    bn = sb("bn2", [P, TILES, 6], F32)
    var = sb("var2", [P, TILES], F32)
    tmp = sb("tmp2", [P, TILES], F32)
    lg = sb("lg", [P, TILES, E], F32)
    ex = sb("ex", [P, TILES, E], F32)
    pr = sb("pr", [P, TILES, E], F32)
    p2 = sb("p2", [P, TILES, E], F32)
    eq = sb("eq", [P, TILES, E], F32)
    sel = sb("sel", [P, 2, TILES, E], F32)
    top = sb("top", [P, 4, TILES], F32)
    w_sb = sb("w_sb", [P, TILES, E], F32)
    wT_sb = sb("wT_sb", [P, WT_GROUPS, P], F32)
    names = ("on_ready", "on_T", "onT_ready", "proj_done", "x_added", "hn_ready", "h_T", "hst_ready", "hh_ready", "hl_ready",
             "logits_done", "lg_ready", "ex_ready", "w_ready", "w_T2", "wT_ready", "w_stored", "bn_chain", "dve_chain3", "y_zero")
    (on_ready, on_T, onT_ready, proj_done, x_added, hn_ready, h_T, hst_ready, hh_ready, hl_ready,
     logits_done, lg_ready, ex_ready, w_ready, w_T2, wT_ready, w_stored, bn_chain, dve_chain, y_zero) = (sem(n) for n in names)

    def bank(kind, s):
        return m.psum[kind * 2 + s]

    with nc.Block() as block:

        @block.vector
        def _(dve):
            c = Chain(dve, dve_chain, 0, CHAIN3)
            c.link(nc.vector.reciprocal(rinv[:, :, :], m.o_sb[:, :, :].rearrange("p t (h d) -> p t h d", h=H)[:, :, :, DH]))

            def norm_o(t):
                for s in range(2):
                    if positive(t * 2 + s - 1):
                        dve.wait_ge(on_T, t * 2 + s - 1)
                    o = m.o_sb[:, seg(t * 2 + s, TB), :].rearrange("p t (h d) -> p t h d", h=H)
                    nc.vector.tensor_tensor(on[:, s, :, :].rearrange("p t (h d) -> p t h d", h=H), o[:, :, :, 0:DH],
                                            rinv[:, seg(t * 2 + s, TB), :].unsqueeze(3).to_broadcast([P, TB, H, DH]), ALU.mult).then_inc(on_ready, 1)

            def residual(t):
                for s in range(2):
                    dve.wait_ge(proj_done, t * 2 + s + 1)
                    xs = m.x_sb[:, seg(t * 2 + s, TB), :]
                    nc.vector.tensor_tensor(xs, bank(1, s)[:, :].rearrange("p (t d) -> p t d", t=TB), xs, ALU.add).then_inc(x_added, 1)

            norm_o(0)
            with dve.Fori(1, B // 2) as t:
                norm_o(t)
                residual(t - 1)
            residual(B // 2 - 1)
            for i in range(TILES):
                if i % TB == 0:
                    dve.wait_ge(x_added, i // TB + 1)
                nc.vector.bn_stats(bn[:, i, :], m.x_sb[:, i, :]).then_inc(bn_chain, 1)
            for i in range(TILES):
                dve.wait_ge(bn_chain, i + 1)
                last = nc.vector.bn_aggr(m.stats[:, i, :], bn[:, i, :])
            c.link(last)
            c.link(nc.vector.tensor_copy(var[:, :], m.stats[:, :, 1]))
            rsqrt_steps(nc, c.link, var[:, :], m.rstd[:, :], tmp[:, :])

            def norm_x(t):
                for s in range(2):
                    if positive(t * 2 + s - 1):
                        dve.wait_ge(h_T, t * 2 + s - 1)
                    for i in range(TB):
                        a = one_of((t * 2 + s) * TB + i)
                        last = nc.vector.tensor_scalar(hn[:, s, i, :], m.x_sb[:, a, :], m.stats[:, a, 0], m.rstd[:, a], ALU.subtract, ALU.mult)
                    last.then_inc(hn_ready, 1)

            def low_and_logits(t):
                for s in range(2):
                    dve.wait_ge(hst_ready, t * 2 + s + 1)
                    dve.wait_ge(hh_ready, t * 2 + s + 1)
                    nc.vector.tensor_tensor(m.xl[:, seg(t * 2 + s, N)], hst[:, s, :], f(m.xh[:, seg(t * 2 + s, N)]), ALU.subtract).then_inc(hl_ready, 1)
                for s in range(2):
                    dve.wait_ge(logits_done, t * 2 + s + 1)
                    nc.vector.tensor_tensor(lg[:, seg(t * 2 + s, TB), :], bank(2, s)[:, 0:TB * E].rearrange("p (t e) -> p t e", e=E),
                                            m.rb_bc[:, :].unsqueeze(1).to_broadcast([P, TB, E]), ALU.add).then_inc(lg_ready, 1)

            norm_x(0)
            with dve.Fori(1, B // 2) as t:
                norm_x(t)
                low_and_logits(t - 1)
            low_and_logits(B // 2 - 1)
            dve.wait_ge(ex_ready, 1)
            c.link(nc.vector.tensor_scalar(ex[:, :, :], ex[:, :, :], 1.0, None, ALU.add))
            c.link(nc.vector.reciprocal(pr[:, :, :], ex[:, :, :]))
            src = pr
            for k in range(2):
                best, first = top[:, 2 * k, :], top[:, 2 * k + 1, :]
                c.link(nc.vector.tensor_reduce(out=best, in_=src[:, :, :], axis=AX.X, op=ALU.max))
                c.link(nc.vector.tensor_tensor(eq[:, :, :], src[:, :, :], best.unsqueeze(2).to_broadcast([P, TILES, E]), ALU.is_equal))
                c.link(nc.vector.tensor_tensor(eq[:, :, :], eq[:, :, :], m.order[:, :, :], ALU.mult))
                c.link(nc.vector.tensor_reduce(out=first, in_=eq[:, :, :], axis=AX.X, op=ALU.max))
                c.link(nc.vector.tensor_tensor(sel[:, k, :, :], m.order[:, :, :], first.unsqueeze(2).to_broadcast([P, TILES, E]), ALU.is_equal))
                if k == 0:
                    c.link(nc.vector.scalar_tensor_tensor(out=p2[:, :, :], in0=sel[:, 0, :, :], scalar=-2.0, in1=pr[:, :, :], op0=ALU.mult, op1=ALU.add))
                    src = p2
            c.link(nc.vector.tensor_tensor(eq[:, :, :], sel[:, 0, :, :], sel[:, 1, :, :], ALU.add))
            c.link(nc.vector.tensor_tensor(eq[:, :, :], eq[:, :, :], pr[:, :, :], ALU.mult))
            c.link(nc.vector.tensor_tensor(top[:, 1, :], top[:, 0, :], top[:, 2, :], ALU.add))
            c.link(nc.vector.reciprocal(top[:, 3, :], top[:, 1, :]))
            nc.vector.tensor_tensor(w_sb[:, :, :], eq[:, :, :], top[:, 3, :].unsqueeze(2).to_broadcast([P, TILES, E]), ALU.mult).then_inc(w_ready, 1)
            c.end()

        @block.tensor
        def _(pe):
            def transpose_o(t):
                for s in range(2):
                    pe.wait_ge(on_ready, t * 2 + s + 1)
                    if positive(t * 2 + s - 1):
                        pe.wait_ge(onT_ready, t * 2 + s - 1)
                    for i in range(TB):
                        last = nc.tensor.transpose(bank(0, s)[:, i * P:(i + 1) * P], on[:, s, i, :], m.ident[:, :])
                    last.then_inc(on_T, 1)

            def project(t):
                for s in range(2):
                    pe.wait_ge(onT_ready, t * 2 + s + 1)
                    if positive(t * 2 + s - 1):
                        pe.wait_ge(x_added, t * 2 + s - 1)
                    for i in range(TB):
                        last = nc.tensor.matmul(bank(1, s)[:, i * P:(i + 1) * P], onT[:, s, i * P:(i + 1) * P], m.wp[:, :], start=True, stop=True)
                    last.then_inc(proj_done, 1)

            def both_o(t):
                transpose_o(t)
                project(t)
            loop(pe, B // 2, both_o)

            def turn(t):
                for s in range(2):
                    pe.wait_ge(hn_ready, t * 2 + s + 1)
                    if positive(t * 2 + s - 1):
                        pe.wait_ge(hh_ready, t * 2 + s - 1)
                    else:
                        pe.wait_ge(onT_ready, B)
                    for i in range(TB):
                        last = nc.tensor.transpose(bank(0, s)[:, i * P:(i + 1) * P], hn[:, s, i, :], m.ident[:, :])
                    last.then_inc(h_T, 1)
                for s in range(2):
                    pe.wait_ge(hst_ready, t * 2 + s + 1)
                    if positive(t * 2 + s - 1):
                        pe.wait_ge(lg_ready, t * 2 + s - 1)
                    for i in range(TB):
                        last = nc.tensor.matmul(bank(2, s)[:, i * E:(i + 1) * E], hst[:, s, i * P:(i + 1) * P], m.rwT[:, :], start=True, stop=True)
                    last.then_inc(logits_done, 1)
            loop(pe, B // 2, turn)
            pe.wait_ge(w_ready, 1)
            for g in range(WT_GROUPS):
                nc.tensor.transpose(bank(3, g)[:, 0:P], w_sb[:, seg(g, P // E), :].rearrange("p t e -> p (t e)"), m.ident[:, :]).then_inc(w_T2, 1)

        @block.scalar
        def _(act):
            def copy_o(t):
                for s in range(2):
                    act.wait_ge(on_T, t * 2 + s + 1)
                    if positive(t * 2 + s - 1):
                        act.wait_ge(proj_done, t * 2 + s - 1)
                    nc.scalar.activation(onT[:, s, :], bank(0, s)[:, :], ACT.Copy).then_inc(onT_ready, 1)
            loop(act, B // 2, copy_o)

            def turn(t):
                for s in range(2):
                    act.wait_ge(h_T, t * 2 + s + 1)
                    if positive(t * 2 + s - 1):
                        act.wait_ge(hl_ready, t * 2 + s - 1)
                    if positive(t * 2 + s - 1):
                        act.wait_ge(logits_done, t * 2 + s - 1)
                    nc.scalar.activation(hst[:, s, :], bank(0, s)[:, :], ACT.Copy).then_inc(hst_ready, 1)
                    nc.scalar.activation(m.xh[:, seg(t * 2 + s, N)], bank(0, s)[:, :], ACT.Copy).then_inc(hh_ready, 1)
            loop(act, B // 2, turn)
            act.wait_ge(lg_ready, B)
            nc.scalar.activation(ex[:, :, :], lg[:, :, :], ACT.Exp, scale=-1.0).then_inc(ex_ready, 1)
            for g in range(WT_GROUPS):
                act.wait_ge(w_T2, g + 1)
                nc.scalar.activation(wT_sb[:, g, :], bank(3, g)[:, 0:P], ACT.Copy).then_inc(wT_ready, 1)

        @block.gpsimd
        def _(pool):
            nc.gpsimd.memset(m.y, 0.0).then_inc(y_zero, 1)
            pool.wait_ge(y_zero, 1)

        @block.sync
        def _(sp):
            for g in range(WT_GROUPS):
                sp.wait_ge(wT_ready, g + 1)
                sp.dma_start(m.w_dram[g * P:(g + 1) * P, :], wT_sb[:, g, :]).then_inc(w_stored, 16)
            sp.wait_ge(w_stored, 16 * WT_GROUPS)


WT_GROUPS = TILES * E // P
CHAIN3 = 1 + 1 + 1 + RSQRT_LINKS + 2 + 11 + 4


def experts(nc, m, ctx):
    sb, sem = tiles(nc, ctx), nc.alloc_semaphore
    wbc = [sb(f"wbc{s}", [P, TOK], F32) for s in range(2)]
    y = m.y
    sg = sb("sg", [P, 2, N], F32)
    yw = sb("yw", [P, 2, N], F32)
    gu = [sb(f"gu{s}", [P, 2, N], F32) for s in range(2)]
    guh = [[sb(f"guh{s}{k}", [P, N], F32R) for k in range(2)] for s in range(2)]
    gul = [[sb(f"gul{s}{k}", [P, N], F32R) for k in range(2)] for s in range(2)]
    yst = sb("yst", [P, 4, N], F32)
    w_loaded = [sem(f"w_loaded{s}") for s in range(2)]
    wbc_loaded = [sem(f"wbc_loaded{s}") for s in range(2)]
    wh_ready = sem("wh_ready")
    w_split = sem("w_split")
    gate_up = sem("gate_up")
    silu_ready = sem("silu_ready")
    gu_ready = sem("gu_ready")
    guh_ready = sem("guh_ready")
    gul_ready = [sem(f"gul_ready{k}") for k in range(2)]
    down_done = sem("down_done")
    yw_ready = sem("yw_ready")
    y_added = sem("y_added")
    yst_ready, y_T, out_ready, out_stored = (sem(n) for n in ("yst_ready", "y_T", "out_ready", "out_stored"))
    GB, UB, YB = (0, 1), (2, 3), 4
    BATCHES = (E + 1) * B

    def sweep(eng, one, between=None):
        def expert(p, slot, last=False):
            for par in range(2):
                one(p, slot, par, par)
            if between and not last:
                between(p + 1, 1 - slot)
            with eng.Fori(1, B // 2) as j:
                for par in range(2):
                    one(p, slot, j * 2 + par, par)
        expert(0, 0)
        expert(1, 1)
        with eng.Fori(0, E // 2 - 1) as q:
            expert(q * 2 + 2, 0)
            expert(q * 2 + 3, 1)
        expert(E, 0, last=True)

    with nc.Block() as block:

        @block.sync
        def _(sp):
            def load(e, p, slot):
                if positive(p - 2):
                    sp.wait_ge(w_split, p - 2)
                ei = slice(e, e + 1) if isinstance(e, int) else bass.ds(e, 1)
                sp.dma_start(m.wraw[:, slot, 0:I], m.gate_w[ei, :, :].rearrange("e h i -> h (e i)")).then_inc(w_loaded[slot], 16)
                sp.dma_start(m.wraw[:, slot, I:2 * I], m.up_w[ei, :, :].rearrange("e h i -> h (e i)")).then_inc(w_loaded[slot], 16)
                sp.dma_start(m.wraw[:, slot, 2 * I:EW].rearrange("p (k d) -> p k d", k=2), m.down_w[ei, :, :].rearrange("e (k p) d -> p (e k) d", p=P)).then_inc(w_loaded[slot], 16)
                if positive(p - 2):
                    sp.wait_ge(yw_ready, (p - 1) * B)
                sp.dma_start(wbc[slot][:, :].rearrange("p (t n) -> p t n", n=P), m.w_dram.rearrange("(t e) n -> e t n", e=E)[ei, :, :].rearrange("e t n -> (e t) n").partition_broadcast(P)).then_inc(wbc_loaded[slot], 16)
            load(0, 1, 1)
            load(1, 2, 0)
            with sp.Fori(1, E // 2) as q:
                load(q * 2, q * 2 + 1, 1)
                load(q * 2 + 1, q * 2 + 2, 0)
            with sp.Fori(0, B) as b:
                sp.wait_ge(out_ready, b + 1)
                sp.dma_start(m.out[bass.ds(b, 1), :, :].rearrange("b (t p) d -> p (b t) d", p=P), m.x_sb[:, seg(b, TB), :]).then_inc(out_stored, 16)
            sp.wait_ge(out_stored, 16 * B)

        @block.gpsimd
        def _(pool):
            def one(p, slot, b, par):
                nb = p * B + b
                pool.wait_ge(guh_ready, nb * 2 + 2)
                if positive(nb - 1):
                    pool.wait_ge(down_done, nb - 1)
                if positive(nb):
                    pool.wait_ge(yw_ready, nb)
                if positive(nb - 1):
                    pool.wait_ge(y_added, nb - 1)
                nc.gpsimd.tensor_tensor(gul[par][1][:, :], gu[par][:, 1, :], f(guh[par][1][:, :]), ALU.subtract).then_inc(gul_ready[1], 1)
                if positive(nb):
                    before = b - 1 if not isinstance(b, int) or b > 0 else B - 1
                    ys = y[:, seg(before, N)]
                    nc.gpsimd.tensor_tensor(ys, ys, yw[:, 1 - par, :], ALU.add).then_inc(y_added, 1)
            sweep(pool, one)
            pool.wait_ge(yw_ready, BATCHES)
            pool.wait_ge(y_added, BATCHES - 1)
            ys = y[:, seg(B - 1, N)]
            nc.gpsimd.tensor_tensor(ys, ys, yw[:, 1, :], ALU.add).then_inc(y_added, 1)

        @block.tensor
        def _(pe):
            def down(slot, n_batch, par):
                if positive(n_batch):
                    pe.wait_ge(yw_ready, n_batch)
                for k in range(2):
                    pe.wait_ge(gul_ready[k], n_batch + 1)
                    w_h = m.wh[slot][:, 2 * I + k * D:2 * I + (k + 1) * D]
                    w_l = m.wl[slot][:, 2 * I + k * D:2 * I + (k + 1) * D]
                    nc.tensor.matmul(m.psum[YB][:, :], w_h, guh[par][k][:, :], start=(k == 0), stop=False)
                    nc.tensor.matmul(m.psum[YB][:, :], w_h, gul[par][k][:, :], start=False, stop=False)
                    last = nc.tensor.matmul(m.psum[YB][:, :], w_l, guh[par][k][:, :], start=False, stop=(k == 1))
                last.then_inc(down_done, 1)

            def one(p, slot, b, par):
                nb = p * B + b
                if isinstance(b, int) and b == 0 and positive(p):
                    pe.wait_ge(w_split, p)
                x_h, x_l = m.xh[:, seg(b, N)], m.xl[:, seg(b, N)]
                for k in range(2):
                    if positive(nb * 2 + k - 1):
                        pe.wait_ge(gu_ready, nb * 2 + k - 1)
                    for c, banks in ((0, GB), (1, UB)):
                        w_h = m.wh[slot][:, c * I + k * P:c * I + (k + 1) * P]
                        w_l = m.wl[slot][:, c * I + k * P:c * I + (k + 1) * P]
                        bank = m.psum[banks[k]][:, :]
                        nc.tensor.matmul(bank, w_h, x_h, start=True, stop=False)
                        nc.tensor.matmul(bank, w_h, x_l, start=False, stop=False)
                        last = nc.tensor.matmul(bank, w_l, x_h, start=False, stop=True)
                    last.then_inc(gate_up, 1)
                if isinstance(b, int) and b == 0:
                    if positive(p):
                        down(1 - slot, nb - 1, 1)
                else:
                    down(slot, nb - 1, 1 - par)
            sweep(pe, one)
            down(0, BATCHES - 1, 1)

            def turn(t):
                for s in range(4):
                    pe.wait_ge(yst_ready, t * 4 + s + 1)
                    if positive(t * 4 + s - 3):
                        pe.wait_ge(out_ready, t * 4 + s - 3)
                    for i in range(TB):
                        last = nc.tensor.transpose(m.psum[s][:, i * P:(i + 1) * P], yst[:, s, i * P:(i + 1) * P], m.ident[:, :])
                    last.then_inc(y_T, 1)
            loop(pe, B // 4, turn)

        @block.scalar
        def _(act):
            def one(p, slot, b, par):
                nb = p * B + b
                for k in range(2):
                    n = nb * 2 + k
                    act.wait_ge(gate_up, n + 1)
                    if positive(n - 1):
                        act.wait_ge(gu_ready, n - 1)
                    nc.scalar.activation(sg[:, k, :], m.psum[GB[k]][:, :], ACT.Silu).then_inc(silu_ready, 1)
                for k in range(2):
                    n = nb * 2 + k
                    act.wait_ge(gu_ready, n + 1)
                    if positive(nb - 1):
                        act.wait_ge(down_done, nb - 1)
                    nc.scalar.activation(guh[par][k][:, :], gu[par][:, k, :], ACT.Copy).then_inc(guh_ready, 1)

            def split_high(p, slot):
                act.wait_ge(w_loaded[slot], (p - 1) // 2 * 48 + 48)
                if positive(p - 1):
                    act.wait_ge(down_done, (p - 1) * B)
                nc.scalar.activation(m.wh[slot][:, :], m.wraw[:, slot, :], ACT.Copy).then_inc(wh_ready, 1)
            sweep(act, one, split_high)

            def turn(t):
                for s in range(4):
                    act.wait_ge(y_added, E * B + t * 4 + s + 1)
                    if positive(t * 4 + s - 3):
                        act.wait_ge(y_T, t * 4 + s - 3)
                    nc.scalar.activation(yst[:, s, :], y[:, seg(t * 4 + s, N)], ACT.Copy).then_inc(yst_ready, 1)
            loop(act, B // 4, turn)

        @block.vector
        def _(dve):
            def weigh_y(p, slot, nb, b, par):
                dve.wait_ge(down_done, nb + 1)
                if isinstance(b, int) and b == 0 and positive(p):
                    dve.wait_ge(wbc_loaded[slot], ((p - 1) // 2) * 16 + 16)
                if positive(nb - 1):
                    dve.wait_ge(y_added, nb - 1)
                weights = wbc[slot][:, seg(b, N)]
                if isinstance(p, int) and p == 0:
                    weights = m.one[:, :].to_broadcast([P, N])
                nc.vector.tensor_tensor(yw[:, par, :], m.psum[YB][:, :], weights, ALU.mult).then_inc(yw_ready, 1)

            def one(p, slot, b, par):
                nb = p * B + b
                for k in range(2):
                    n = nb * 2 + k
                    dve.wait_ge(silu_ready, n + 1)
                    if positive(nb - 1):
                        dve.wait_ge(gul_ready[k], nb - 1)
                    nc.vector.tensor_tensor(gu[par][:, k, :], m.psum[UB[k]][:, :], sg[:, k, :], ALU.mult).then_inc(gu_ready, 1)
                dve.wait_ge(guh_ready, nb * 2 + 1)
                if positive(nb - 1):
                    dve.wait_ge(down_done, nb - 1)
                nc.vector.tensor_tensor(gul[par][0][:, :], gu[par][:, 0, :], f(guh[par][0][:, :]), ALU.subtract).then_inc(gul_ready[0], 1)
                if isinstance(b, int) and b == 0:
                    if positive(p):
                        weigh_y(p - 1, 1 - slot, nb - 1, B - 1, 1 - par)
                else:
                    weigh_y(p, slot, nb - 1, b - 1, 1 - par)

            def split_low(p, slot):
                dve.wait_ge(wh_ready, p)
                nc.vector.tensor_tensor(m.wl[slot][:, :], m.wraw[:, slot, :], f(m.wh[slot][:, :]), ALU.subtract).then_inc(w_split, 1)
            sweep(dve, one, split_low)
            weigh_y(E, 0, BATCHES - 1, B - 1, 1)

            def turn(t):
                for s in range(4):
                    dve.wait_ge(y_T, t * 4 + s + 1)
                    xs = m.x_sb[:, seg(t * 4 + s, TB), :]
                    nc.vector.tensor_tensor(xs, m.psum[s][:, :].rearrange("p (t d) -> p t d", t=TB), xs, ALU.add).then_inc(out_ready, 1)
            loop(dve, B // 4, turn)


def layer(nc, io):
    m = Mem(nc, io)
    for phase in (prepare, attention, after_attention, experts):
        with ExitStack() as ctx:
            phase(nc, m, ctx)


_INS = {"L0_attn_x": "x", "L0_attn_Wkqv": "Wkqv", "L0_attn_bkqv": "bkqv", "L0_attn_Wp": "Wp", "L0_attn_bp": "bp",
        "L0_ffn_shared_gate": "shared_gate", "L0_ffn_shared_up": "shared_up", "L0_ffn_shared_down": "shared_down",
        "L0_ffn_gate_w": "gate_w", "L0_ffn_up_w": "up_w", "L0_ffn_down_w": "down_w",
        "L0_ffn_router_w": "router_w", "L0_ffn_routing_bias": "routing_bias"}


def kernel(**inputs):
    import concourse.bacc as bacc
    from concourse.bass_utils import run_bass_kernel_spmd as run

    nc = bacc.Bacc("TRN2", target_bir_lowering=False, num_devices=1)
    arrays, io = {}, []
    for name, short in _INS.items():
        a = np.ascontiguousarray(inputs[name])
        arrays[f"in_{short}"] = a
        io.append(nc.dram_tensor(f"in_{short}", a.shape, mybir.dt.from_np(a.dtype), kind="ExternalInput").ap())
    io.append(nc.dram_tensor("out", (B, N, D), F32, kind="ExternalOutput").ap())
    io.append(nc.dram_tensor("w_dram", (TILES * E, P), F32, kind="Internal").ap())
    layer(nc, io)
    r = run(nc, [arrays], core_ids=[0])
    return r.results[0]["out"]
```
